# Optimizing a Trainium2 kernel written in Bass

```python
import numpy as np
import jax
import jax.numpy as jnp

def _softmax(x, axis=-1):
    return jax.nn.softmax(x, axis=axis)

def _gelu(x):
    return jax.nn.gelu(x, approximate=True)

def _silu(x):
    return jax.nn.silu(x)

def _sigmoid(x):
    return jax.nn.sigmoid(x)

def _layernorm(x, axis=-1, eps=1e-05):
    m = jnp.mean(x, axis=axis, keepdims=True)
    v = jnp.var(x, axis=axis, keepdims=True)
    return (x - m) / jnp.sqrt(v + eps)

def _scatter_add(tgt, idx, src, axis=0):
    return tgt.at[idx].add(src)

def _segment_sum(src, seg, n):
    return jax.ops.segment_sum(src, seg, n)
kernel_name = 'mk_adaln_attn_ffn_d1_seqx_r8_ec3b6a'

def setup_inputs(seed: int=0):
    np.random.seed(seed)
    _w = jnp.asarray

    def _rec_inputs():
        import jax
        import jax.numpy as jnp
        _rk = jax.random.key(seed)
        x = 8.748e-05 + 1 * jax.random.normal(jax.random.fold_in(_rk, 1), (8, 128, 256), jnp.float32)
        _lenS = 128 - jax.random.randint(jax.random.fold_in(_rk, 7), (8,), 0, max(1, 128 // 4) + 1, jnp.int32)
        _lenS2 = 128 - jax.random.randint(jax.random.fold_in(_rk, 8), (8,), 0, max(1, 128 // 4) + 1, jnp.int32)
        cond_2048 = -9.80646e-05 + 1.00041 * jax.random.normal(jax.random.fold_in(_rk, 11), (8, 256), jnp.float32)
        return (x, cond_2048)
    x, cond_2048 = _rec_inputs()

    def _L0_cond_setup():
        import jax, jax.numpy as jnp
        import numpy as np
        DT = 0.01
        EPSILON = 0.08
        ALPHA = 0.7
        BETA = 0.8
        CLAMP = 20.0
        B, T, N = (32, 128, 256)

        def _derivative(q, p, drive, coupling, bias):
            i_couple = jnp.tanh(q) @ coupling.T
            dq = q - q ** 3 / 3.0 - p + drive + i_couple + bias
            dp = EPSILON * (q + ALPHA - BETA * p)
            return (dq, dp)

        def _rk4_step(q, p, drive, coupling, bias):
            dq1, dp1 = _derivative(q, p, drive, coupling, bias)
            dq2, dp2 = _derivative(q + 0.5 * DT * dq1, p + 0.5 * DT * dp1, drive, coupling, bias)
            dq3, dp3 = _derivative(q + 0.5 * DT * dq2, p + 0.5 * DT * dp2, drive, coupling, bias)
            dq4, dp4 = _derivative(q + DT * dq3, p + DT * dp3, drive, coupling, bias)
            q_next = q + DT / 6.0 * (dq1 + 2 * dq2 + 2 * dq3 + dq4)
            p_next = p + DT / 6.0 * (dp1 + 2 * dp2 + 2 * dp3 + dp4)
            q_next = jnp.clip(q_next, -CLAMP, CLAMP)
            p_next = jnp.clip(p_next, -CLAMP, CLAMP)
            return (q_next, p_next)
        key = jax.random.key(seed)
        k1, k2, k3, k4 = jax.random.split(key, 4)
        return {'q0': jax.random.normal(k1, (B, N), dtype=jnp.float32), 'p0': jax.random.normal(k2, (B, N), dtype=jnp.float32), 'input_drive_seq': jax.random.normal(k3, (B, T, N), dtype=jnp.float32), 'coupling': jax.random.normal(k4, (N, N), dtype=jnp.float32) * 0.01, 'bias': jnp.zeros((N,), dtype=jnp.float32)}
    _L0_cond_all = _L0_cond_setup()
    _L0_cond_in = {k: v for k, v in _L0_cond_all.items() if k in ('coupling', 'bias')}
    del _L0_cond_all

    def _L0_attn_setup():
        import jax, jax.numpy as jnp
        import numpy as np
        HIDDEN = 256
        KEY = 256
        EPS = 1e-05
        key = jax.random.key(seed)
        k1, k2, k3 = jax.random.split(key, 3)
        B, S = (4, 256)
        x = jax.random.normal(k1, (B, S, HIDDEN), dtype=jnp.float32)
        bq = 1.0 / np.sqrt(HIDDEN)
        qkv = jax.random.uniform(k2, (HIDDEN, KEY * 3), minval=-bq, maxval=bq, dtype=jnp.float32)
        bo = 1.0 / np.sqrt(KEY)
        o_proj = jax.random.uniform(k3, (KEY, HIDDEN), minval=-bo, maxval=bo, dtype=jnp.float32)
        gamma = jnp.ones((HIDDEN,), dtype=jnp.float32)
        beta = jnp.zeros((HIDDEN,), dtype=jnp.float32)
        return {'x': x, 'qkv': qkv, 'o_proj': o_proj, 'gamma': gamma, 'beta': beta}
    _L0_attn_all = _L0_attn_setup()
    _L0_attn_in = {k: v for k, v in _L0_attn_all.items() if k in ('qkv', 'o_proj', 'gamma', 'beta')}
    del _L0_attn_all

    def _L0_cond2_setup():
        import math
        import jax, jax.numpy as jnp
        import numpy as np
        ENCODER_SIZE = 128
        NUM_HEADER = 16
        DK = ENCODER_SIZE // NUM_HEADER
        B, S = (4, 256)
        key = jax.random.key(seed)
        kx, km, kq, kk, kv, ko = jax.random.split(key, 6)
        x = jax.random.normal(kx, (B, ENCODER_SIZE, S), dtype=jnp.float32)
        mask = (jax.random.uniform(km, (B, S)) < 0.9).astype(jnp.float32)
        lim = math.sqrt(6.0 / (ENCODER_SIZE + DK))
        Wq = jax.random.uniform(kq, (NUM_HEADER, ENCODER_SIZE, DK), minval=-lim, maxval=lim, dtype=jnp.float32)
        Wk = jax.random.uniform(kk, (NUM_HEADER, ENCODER_SIZE, DK), minval=-lim, maxval=lim, dtype=jnp.float32)
        Wv = jax.random.uniform(kv, (NUM_HEADER, ENCODER_SIZE, DK), minval=-lim, maxval=lim, dtype=jnp.float32)
        limo = math.sqrt(6.0 / ENCODER_SIZE)
        Wo = jax.random.uniform(ko, (ENCODER_SIZE, ENCODER_SIZE), minval=-limo, maxval=limo, dtype=jnp.float32)
        return {'x': x, 'mask': mask, 'Wq': Wq, 'Wk': Wk, 'Wv': Wv, 'Wo': Wo}
    _L0_cond2_all = _L0_cond2_setup()
    _L0_cond2_in = {k: v for k, v in _L0_cond2_all.items() if k in ('Wq', 'Wk', 'Wv', 'Wo')}
    del _L0_cond2_all

    def _L0_ffn_setup():
        import jax, jax.numpy as jnp
        import numpy as np
        HIDDEN = 256
        INTER = 1024
        BATCH, LOCAL_SEQ = (2, 512)
        key = jax.random.key(seed)
        k1, k2, k3 = jax.random.split(key, 3)
        h_shard = jax.random.normal(k1, (BATCH, LOCAL_SEQ, HIDDEN), dtype=jnp.float32)
        w_gate_up = jax.random.normal(k2, (2 * INTER, HIDDEN), dtype=jnp.float32) * 0.02
        w_down = jax.random.normal(k3, (HIDDEN, INTER), dtype=jnp.float32) * 0.02
        return {'h_shard': h_shard, 'w_gate_up': w_gate_up, 'w_down': w_down}
    _L0_ffn_all = _L0_ffn_setup()
    _L0_ffn_in = {k: v for k, v in _L0_ffn_all.items() if k in ('w_gate_up', 'w_down')}
    del _L0_ffn_all
    return {'x': x, 'cond_2048': cond_2048, 'L0_cond_coupling': _L0_cond_in['coupling'], 'L0_cond_bias': _L0_cond_in['bias'], 'L0_attn_qkv': _L0_attn_in['qkv'], 'L0_attn_o_proj': _L0_attn_in['o_proj'], 'L0_attn_gamma': _L0_attn_in['gamma'], 'L0_attn_beta': _L0_attn_in['beta'], 'L0_cond2_Wq': _L0_cond2_in['Wq'], 'L0_cond2_Wk': _L0_cond2_in['Wk'], 'L0_cond2_Wv': _L0_cond2_in['Wv'], 'L0_cond2_Wo': _L0_cond2_in['Wo'], 'L0_ffn_w_gate_up': _L0_ffn_in['w_gate_up'], 'L0_ffn_w_down': _L0_ffn_in['w_down']}

def reference(x, cond_2048, L0_cond_coupling, L0_cond_bias, L0_attn_qkv, L0_attn_o_proj, L0_attn_gamma, L0_attn_beta, L0_cond2_Wq, L0_cond2_Wk, L0_cond2_Wv, L0_cond2_Wo, L0_ffn_w_gate_up, L0_ffn_w_down):
    import jax
    import jax.numpy as jnp

    def _L0_cond_ref(q0, p0, input_drive_seq, coupling, bias):
        import jax, jax.numpy as jnp
        import numpy as np
        DT = 0.01
        EPSILON = 0.08
        ALPHA = 0.7
        BETA = 0.8
        CLAMP = 20.0
        B, T, N = (32, 128, 256)

        def _derivative(q, p, drive, coupling, bias):
            i_couple = jnp.tanh(q) @ coupling.T
            dq = q - q ** 3 / 3.0 - p + drive + i_couple + bias
            dp = EPSILON * (q + ALPHA - BETA * p)
            return (dq, dp)

        def _rk4_step(q, p, drive, coupling, bias):
            dq1, dp1 = _derivative(q, p, drive, coupling, bias)
            dq2, dp2 = _derivative(q + 0.5 * DT * dq1, p + 0.5 * DT * dp1, drive, coupling, bias)
            dq3, dp3 = _derivative(q + 0.5 * DT * dq2, p + 0.5 * DT * dp2, drive, coupling, bias)
            dq4, dp4 = _derivative(q + DT * dq3, p + DT * dp3, drive, coupling, bias)
            q_next = q + DT / 6.0 * (dq1 + 2 * dq2 + 2 * dq3 + dq4)
            p_next = p + DT / 6.0 * (dp1 + 2 * dp2 + 2 * dp3 + dp4)
            q_next = jnp.clip(q_next, -CLAMP, CLAMP)
            p_next = jnp.clip(p_next, -CLAMP, CLAMP)
            return (q_next, p_next)
        drive_tbn = jnp.swapaxes(input_drive_seq, 0, 1)

        def scan_fn(carry, drive):
            q, p = carry
            q, p = _rk4_step(q, p, drive, coupling, bias)
            return ((q, p), q)
        (_, _), q_trace_tbn = jax.lax.scan(scan_fn, (q0, p0), drive_tbn)
        return jnp.swapaxes(q_trace_tbn, 0, 1)

    def _L0_attn_ref(x, qkv, o_proj, gamma, beta):
        import jax, jax.numpy as jnp
        import numpy as np
        HIDDEN = 256
        KEY = 256
        EPS = 1e-05
        residual = x
        mu = jnp.mean(x, axis=-1, keepdims=True)
        var = jnp.mean((x - mu) ** 2, axis=-1, keepdims=True)
        x_norm = (x - mu) / jnp.sqrt(var + EPS) * gamma + beta
        q = x_norm @ qkv[:, :KEY]
        k = x_norm @ qkv[:, KEY:2 * KEY]
        v = x_norm @ qkv[:, 2 * KEY:]
        scale = 1.0 / jnp.sqrt(jnp.float32(KEY))
        scores = jnp.einsum('bsk,btk->bst', q, k) * scale
        S_len = x.shape[1]
        causal = jnp.tril(jnp.ones((S_len, S_len), dtype=bool))
        scores = jnp.where(causal[None], scores, -jnp.inf)
        attn = jax.nn.softmax(scores, axis=-1)
        out = attn @ v
        out = out @ o_proj
        return out + residual

    def _L0_cond2_ref(x, mask, Wq, Wk, Wv, Wo):
        import math
        import jax, jax.numpy as jnp
        import numpy as np
        ENCODER_SIZE = 128
        NUM_HEADER = 16
        DK = ENCODER_SIZE // NUM_HEADER
        B, S = (4, 256)
        num_header = Wq.shape[0]
        dk = Wq.shape[2]
        sqrt_dk_inv = 1.0 / math.sqrt(dk)
        xt = jnp.transpose(x, (0, 2, 1))
        q = xt @ Wq[1]
        k = xt @ Wk[1]
        v = xt @ Wv[1]
        scores = jnp.einsum('bqd,bkd->bqk', q, k) * sqrt_dk_inv
        hmask = mask[:, None, :]
        vmask = mask[:, :, None]
        scores = scores * hmask + (1.0 - hmask) * -1e+30
        attn = jax.nn.softmax(scores, axis=2) * vmask
        head = attn @ v
        heads = jnp.tile(head, (1, 1, num_header))
        out = heads @ Wo
        return jnp.transpose(out, (0, 2, 1))

    def _L0_ffn_ref(h_shard, w_gate_up, w_down):
        import jax, jax.numpy as jnp
        import numpy as np
        HIDDEN = 256
        INTER = 1024
        BATCH, LOCAL_SEQ = (2, 512)
        batch, local_seq, hidden = h_shard.shape
        gate_up = jnp.einsum('bsh,oh->bso', h_shard, w_gate_up)
        gate, up = jnp.split(gate_up, 2, axis=-1)
        h = jax.nn.silu(gate) * up
        out = jnp.einsum('bsi,hi->bsh', h, w_down)
        return out
    x = x + _L0_attn_ref(_L0_cond_ref(cond_2048, cond_2048, x, L0_cond_coupling, L0_cond_bias), L0_attn_qkv, L0_attn_o_proj, L0_attn_gamma, L0_attn_beta)
    x = x + _L0_ffn_ref(_L0_cond2_ref(x, cond_2048, L0_cond2_Wq, L0_cond2_Wk, L0_cond2_Wv, L0_cond2_Wo), L0_ffn_w_gate_up, L0_ffn_w_down)
    return x

_drawn_inputs = setup_inputs


def setup_inputs(seed=0):
    import zlib

    import numpy as np

    out = dict(_drawn_inputs(seed))
    spreads = {'L0_cond_bias': (0.0, 0.1), 'L0_attn_gamma': (1.0, 0.2), 'L0_attn_beta': (0.0, 0.316)}
    factors = {}
    for name, (base, spread) in spreads.items():
        noise = np.random.default_rng([zlib.crc32(name.encode()), seed]).standard_normal(out[name].shape)
        drawn = base * np.exp(spread * noise) if base else spread * noise
        out[name] = jnp.asarray(drawn.astype(out[name].dtype))
    for name, factor in factors.items():
        out[name] = (out[name] * factor).astype(out[name].dtype)
    return out
```

```python
from contextlib import ExitStack

import concourse.bass as bass
from concourse import mybir

P = 128
B, T, N = 8, 128, 256
NC = N // P
COLS = NC * B
TOK = B * T
HALF = 512
INTER = 1024
NJ = INTER // P
HEADS, DK = 16, 8

DT = 0.01
EPS_P = 0.08
ALPHA, BETA, CLAMP = 0.7, 0.8, 20.0
P_SHIFT = ALPHA / BETA
E2 = 0.5 * DT * EPS_P
LN_EPS = 1e-5
NEG = -1e30
MASKED = -3e38

STEP = [0.5 * DT, 0.5 * DT, DT, DT / 6.0]
LINEAR = [0.5 * DT, 0.5 * DT, DT, 1.0 / 3.0 + DT / 6.0]
CUBIC = [0.5 * DT / 3.0, 0.5 * DT / 3.0, DT / 3.0, DT / 18.0]

ALU = mybir.AluOpType
ACT = mybir.ActivationFunctionType
F32 = mybir.dt.float32
F16 = mybir.dt.float16
U32 = mybir.dt.uint32
AX_X = mybir.AxisListType.X
EXPONENT = 0x7F800000


def fhn_attention_ffn(nc, x_feat, x_tok, cond_feat, cond_row, coupling_t, bias, wq_t, wk_t, wv_t,
                      wo, gamma, beta, wq2_t, wk2_t, wv2_t, wo2, w_gate_up_t, w_down_t, out):
    with ExitStack() as ctx:
        def sb(name, shape, dt=F32):
            return ctx.enter_context(nc.sbuf_tensor(name, shape, dt))

        def sem(name):
            return ctx.enter_context(nc.semaphore(name))

        psum = ctx.enter_context(nc.psum_tensor("psum", [P, 8, HALF], F32))

        hid = sb("hid", [P, NJ, TOK])
        shared = hid[:, :, :].rearrange("p (a h) n -> p a (h n)", h=2)
        xf = shared[:, 0, :].rearrange("p (t c) -> p t c", c=COLS)
        qtok = shared[:, 1, :].rearrange("p (b n) -> p b n", b=B)
        xn = shared[:, 2, :].rearrange("p (b n) -> p b n", b=B)
        z = shared[:, 3, :].rearrange("p (c n) -> p c n", c=NC)
        xt = sb("xt", [P, B, N])
        cf = sb("cf", [P, COLS])
        ct = sb("ct", [P, NC, N])
        bias_sb = sb("bias_sb", [P, NC])
        wqt = sb("wqt", [P, NC, N])
        wkt = sb("wkt", [P, NC, N])
        wvt = sb("wvt", [P, NC, N])
        wo_sb = sb("wo_sb", [P, NC, N])
        gam = sb("gam", [P, NC])
        bet = sb("bet", [P, NC])
        hm = sb("hm", [P, B, N])
        wq2 = sb("wq2", [DK, P])
        wk2 = sb("wk2", [DK, P])
        wv2 = sb("wv2", [P, P])
        wo2_sb = sb("wo2_sb", [P, P])
        wgu = sb("wgu", [P, NC, 2 * INTER])
        wd = sb("wd", [P, NJ, N])

        ident = sb("ident", [P, P])
        causal = sb("causal", [P, T])

        cmax = sb("cmax", [P, 1])
        call = sb("call", [P, 1])
        cclip = sb("cclip", [P, 1])
        cexp = sb("cexp", [P, 1])
        cinv = sb("cinv", [P, 1])
        cscaled = sb("cscaled", [P, NC, N])
        c_hi = sb("c_hi", [P, NC, N], F16)
        c_lo = sb("c_lo", [P, NC, N], F16)
        gain = sb("gain", [P, 4])

        bias_d = sb("bias_d", [P, NC])
        drive = sb("drive", [P, T + 1, COLS])
        q = sb("q", [P, 4, COLS])
        qc = sb("qc", [P, COLS])
        p1 = sb("p1", [P, COLS])
        pu = sb("pu", [P, COLS])
        ps_ = sb("ps_", [P, COLS])
        p2 = sb("p2", [P, COLS])
        p3 = sb("p3", [P, COLS])
        p4 = sb("p4", [P, COLS])
        y = sb("y", [P, 4, COLS])
        g = sb("g", [P, 4, COLS])
        bq = sb("bq", [P, COLS])
        r3 = sb("r3", [P, COLS])
        v1 = sb("v1", [P, COLS])
        v2 = sb("v2", [P, COLS])
        v3 = sb("v3", [P, COLS])
        s1 = sb("s1", [P, COLS])
        s2 = sb("s2", [P, COLS])
        u = sb("u", [P, 4, COLS])
        base = sb("base", [P, 4, COLS])
        th = sb("th", [P, COLS])
        th_hi = sb("th_hi", [P, COLS], F16)
        th_lo = sb("th_lo", [P, COLS], F16)
        sq = sb("sq", [P, 4, COLS])
        trace = sb("trace", [P, T, COLS])

        wqk = sb("wqk", [P, NC, N])
        wvo = sb("wvo", [P, NC, N])
        resid = sb("resid", [P, B, N])
        stats = sb("stats", [P, B, 6])
        mv = sb("mv", [P, B, 2])
        vare = sb("vare", [P, B])
        std = sb("std", [P, B])
        rstd = sb("rstd", [P, B])
        xnt = sb("xnt", [P, NC, TOK])
        vo = sb("vo", [P, B, N])
        sm = sb("sm", [P, B, T])
        nmax = sb("nmax", [P, B])
        ex = sb("ex", [P, B, T])
        rsum = sb("rsum", [P, B])
        rinv = sb("rinv", [P, B])
        ext = sb("ext", [P, B, T])
        x1 = sb("x1", [P, B, N])

        a2 = sb("a2", [P, P])
        wvo2 = sb("wvo2", [P, P])
        km = sb("km", [P, B, N])
        x1h = sb("x1h", [P, B, N])
        z2 = sb("z2", [P, B, N])
        vo2 = sb("vo2", [P, B, NC, P])
        sm2 = sb("sm2", [P, 2, NC, N])
        max2 = sb("max2", [P, B, NC])
        nmax2 = sb("nmax2", [P, B, NC])
        ex2 = sb("ex2", [P, 2, NC, N])
        sum2 = sb("sum2", [P, B, NC])
        inv2 = sb("inv2", [P, B, NC])
        r2 = sb("r2", [P, B, NC])
        ext2 = sb("ext2", [P, 2, NC, N])
        ht = xnt

        sg = sb("sg", [P, 2, HALF])
        yout = xt

        ct_in = sem("ct_in")
        cond_in = sem("cond_in")
        bias_in = sem("bias_in")
        xf_in = sem("xf_in")
        attn_in = sem("attn_in")
        xt_in = sem("xt_in")
        hm_in = sem("hm_in")
        w2_in = sem("w2_in")
        ffn_in = sem("ffn_in")
        zeroed = sem("zeroed")
        consts = sem("consts")
        cmax_done = sem("cmax_done")
        call_done = sem("call_done")
        cprep = sem("cprep")
        c_split = sem("c_split")
        bias_done = sem("bias_done")
        drive_done = sem("drive_done")
        gain_done = sem("gain_done")

        q_ready = [sem(f"q_ready{s}") for s in range(4)]
        clip_ready = sem("clip_ready")
        pu_ready = sem("pu_ready")
        hi_ready = [sem(f"hi_ready{s}") for s in range(4)]
        tanh_ready = [sem(f"tanh_ready{s}") for s in range(4)]
        square_ready = [sem(f"square_ready{s}") for s in range(4)]
        lo_ready = [sem(f"lo_ready{s}") for s in range(4)]
        coupled = [sem(f"coupled{s}") for s in range(4)]
        linear_ready = [sem(f"linear_ready{s}") for s in range(4)]
        cubic_ready = [sem(f"cubic_ready{s}") for s in range(4)]
        base_ready = [sem(f"base_ready{s}") for s in range(4)]
        p_ready = [sem(f"p_ready{s}") for s in range(4)]
        g_ready = sem("g_ready")
        saved = sem("saved")

        folded = sem("folded")
        folded_out = sem("folded_out")
        km_done = sem("km_done")
        tq_ready = sem("tq_ready")
        tq_copied = sem("tq_copied")
        resid_done = sem("resid_done")
        stats_done = sem("stats_done")
        mv_done = sem("mv_done")
        var_done = sem("var_done")
        std_done = sem("std_done")
        rstd_done = sem("rstd_done")
        xn_done = sem("xn_done")
        xnt_psum = sem("xnt_psum")
        xnt_dve = sem("xnt_dve")
        xnt_act = sem("xnt_act")
        z_psum = sem("z_psum")
        z_dve = sem("z_dve")
        z_act = sem("z_act")
        vo_psum = sem("vo_psum")
        vo_dve = sem("vo_dve")
        vo_act = sem("vo_act")
        s_psum = sem("s_psum")
        sm_done = sem("sm_done")
        nmax_done = sem("nmax_done")
        ex_done = sem("ex_done")
        rinv_done = sem("rinv_done")
        ext_psum = sem("ext_psum")
        ext_dve = sem("ext_dve")
        ext_act = sem("ext_act")
        o_psum = sem("o_psum")
        x1_done = sem("x1_done")
        x1h_done = sem("x1h_done")
        z2_psum = sem("z2_psum")
        z2_dve = sem("z2_dve")
        z2_act = sem("z2_act")
        vo2_psum = sem("vo2_psum")
        vo2_dve = sem("vo2_dve")
        vo2_act = sem("vo2_act")
        s2_psum = sem("s2_psum")
        sm2_done = sem("sm2_done")
        nmax2_done = sem("nmax2_done")
        ex2_done = sem("ex2_done")
        inv2_done = sem("inv2_done")
        r2_done = sem("r2_done")
        ext2_psum = sem("ext2_psum")
        ext2_done = sem("ext2_done")
        h_psum = sem("h_psum")
        h_done = sem("h_done")
        gu_psum = sem("gu_psum")
        silu_done = sem("silu_done")
        hid_done = sem("hid_done")
        y_psum = sem("y_psum")
        y_done = sem("y_done")
        out_done = sem("out_done")

        block = ctx.enter_context(nc.Block())

        @block.sync
        def _(sp):
            sp.dma_start(ct[:, :, :], coupling_t).then_inc(ct_in, 16)
            sp.dma_start(cf[:, :], cond_feat).then_inc(cond_in, 16)
            sp.dma_start(bias_sb[:, :], bias).then_inc(bias_in, 16)
            sp.dma_start(xf[:, :, :], x_feat).then_inc(xf_in, 16)
            for dst, src in ((wqt, wq_t), (wkt, wk_t), (wvt, wv_t), (wo_sb, wo)):
                sp.dma_start(dst[:, :, :], src).then_inc(attn_in, 16)
            for dst, src in ((gam, gamma), (bet, beta)):
                sp.dma_start(dst[:, :], src).then_inc(attn_in, 16)
            sp.dma_start(wq2[:, :], wq2_t).then_inc(w2_in, 16)
            sp.dma_start(wk2[:, :], wk2_t).then_inc(w2_in, 16)
            sp.dma_start(wo2_sb[:, :], wo2).then_inc(w2_in, 16)
            for h in range(HEADS):
                sp.dma_start(wv2[h * DK:(h + 1) * DK, :], wv2_t).then_inc(w2_in, 16)
            sp.dma_start(hm[:, :, :].rearrange("p b n -> p (b n)"),
                         cond_row.partition_broadcast(P)).then_inc(hm_in, 16)
            sp.dma_start(xt[:, :, :], x_tok).then_inc(xt_in, 16)
            sp.dma_start(wgu[:, :, :], w_gate_up_t).then_inc(ffn_in, 16)
            sp.dma_start(wd[:, :, :], w_down_t).then_inc(ffn_in, 16)
            for b in range(B):
                sp.wait_ge(y_done, b + 1)
                sp.dma_start(out[b, :, :], yout[:, b, :]).then_inc(out_done, 16)
            sp.wait_ge(out_done, 16 * B)

        @block.gpsimd
        def _(pool):
            nc.gpsimd.memset(ident[:, :], 0.0).then_inc(zeroed, 1)
            nc.gpsimd.memset(causal[:, :], 0.0).then_inc(zeroed, 1)
            pool.wait_ge(cmax_done, 1)
            nc.gpsimd.partition_all_reduce(call[:, :], cmax[:, :], P,
                                           bass.bass_isa.ReduceOp.max).then_inc(call_done, 1)
            pool.wait_ge(zeroed, 2)
            nc.gpsimd.affine_select(out=ident[:, :], in_=ident[:, :], compare_op=ALU.not_equal, fill=1.0,
                                    base=0, pattern=[[-1, P]], channel_multiplier=1).then_inc(consts, 1)
            nc.gpsimd.affine_select(out=causal[:, :], in_=causal[:, :], compare_op=ALU.is_ge, fill=MASKED,
                                    base=0, pattern=[[-1, T]], channel_multiplier=1).then_inc(consts, 1)
            pool.wait_ge(hm_in, 16)
            nc.gpsimd.tensor_scalar(km[:, :, :], hm[:, :, :], -1.0, 1.0, ALU.mult, ALU.add).then_inc(km_done, 1)
            pool.wait_ge(km_done, 1)
            nc.gpsimd.tensor_scalar(km[:, :, :], km[:, :, :], NEG, 1.0, ALU.mult, ALU.mult).then_inc(km_done, 1)
            pool.sem_inc(saved, 1)
            with pool.Fori(0, T) as t:
                pool.wait_ge(clip_ready, t + 2)
                nc.gpsimd.tensor_copy(trace[:, bass.ds(t, 1), :].rearrange("p a c -> p (a c)"),
                                      qc[:, :]).then_inc(saved, 1)
            pool.wait_ge(xt_in, 16)
            for i in range(4):
                pool.wait_ge(tq_copied, i + 1)
                nc.gpsimd.tensor_tensor(resid[:, 2 * i:2 * i + 2, :], xt[:, 2 * i:2 * i + 2, :],
                                        qtok[:, 2 * i:2 * i + 2, :], ALU.add).then_inc(resid_done, 1)

        @block.scalar
        def _(act):
            act.wait_ge(xf_in, 16)
            act.wait_ge(bias_done, 2)
            for c in range(NC):
                nc.scalar.activation(drive[:, 0:T, c * B:(c + 1) * B], xf[:, :, c * B:(c + 1) * B],
                                     ACT.Identity, bias=bias_d[:, c:c + 1],
                                     scale=0.5 * DT).then_inc(drive_done, 1)
            with act.Fori(0, T) as t:
                for s in range(4):
                    act.wait_ge(q_ready[s], t + 1)
                    nc.scalar.activation(th_hi[:, :], q[:, s, :], ACT.Tanh).then_inc(hi_ready[s], 1)
                    nc.scalar.activation(th[:, :], q[:, s, :], ACT.Tanh).then_inc(tanh_ready[s], 1)
                    if s == 0:
                        act.wait_ge(clip_ready, t + 1)
                    nc.scalar.activation(sq[:, s, :], qc[:, :] if s == 0 else q[:, s, :], ACT.Square,
                                         scale=CUBIC[s] ** 0.5).then_inc(square_ready[s], 1)

            for i in range(4):
                act.wait_ge(tq_ready, i + 1)
                nc.scalar.activation(qtok[:, 2 * i:2 * i + 2, :].rearrange("p a n -> p (a n)"),
                                     psum[:, i, :], ACT.Copy).then_inc(tq_copied, 1)
            act.wait_ge(var_done, 1)
            nc.scalar.activation(std[:, :], vare[:, :], ACT.Sqrt).then_inc(std_done, 1)
            act.wait_ge(attn_in, 16 * 6)
            for i in range(2):
                act.wait_ge(xnt_psum, i + 1)
                nc.scalar.activation(xnt[:, 1, i * HALF:(i + 1) * HALF], psum[:, 6 + i, :], ACT.Identity,
                                     bias=bet[:, 1:2], scale=gam[:, 1:2]).then_inc(xnt_act, 1)
            for i in range(2):
                act.wait_ge(z_psum, 2 * i + 2)
                nc.scalar.activation(z[:, 1, i * HALF:(i + 1) * HALF], psum[:, 2 + i, :],
                                     ACT.Copy).then_inc(z_act, 1)
            for i in range(2):
                act.wait_ge(vo_psum, 2 * i + 2)
                nc.scalar.activation(vo[:, 4 * i + 2:4 * i + 4, :].rearrange("p a n -> p (a n)"),
                                     psum[:, 5 + 2 * i, :], ACT.Copy).then_inc(vo_act, 1)
            for b in range(B):
                act.wait_ge(nmax_done, b // 4 + 1)
                nc.scalar.activation(ex[:, b, :], sm[:, b, :], ACT.Exp, bias=nmax[:, b:b + 1],
                                     accum_out=rsum[:, b:b + 1]).then_inc(ex_done, 1)
            act.wait_ge(ext_psum, 2)
            nc.scalar.activation(ext[:, 4:8, :].rearrange("p a n -> p (a n)"), psum[:, 3, :],
                                 ACT.Copy).then_inc(ext_act, 1)
            for i in range(4):
                act.wait_ge(z2_psum, i + 1)
                nc.scalar.activation(z2[:, 2 * i:2 * i + 2, :].rearrange("p a n -> p (a n)"),
                                     psum[:, i, :], ACT.Copy).then_inc(z2_act, 1)
            for i in range(4):
                act.wait_ge(vo2_psum, i + 1)
                nc.scalar.activation(vo2[:, 2 * i:2 * i + 2, :, :].rearrange("p a c n -> p (a c n)"),
                                     psum[:, 4 + i, :], ACT.Copy).then_inc(vo2_act, 1)
            for b in range(B):
                act.wait_ge(nmax2_done, b + 1)
                if b >= 2:
                    act.wait_ge(ext2_psum, b - 1)
                for c in range(NC):
                    nc.scalar.activation(ex2[:, b % 2, c, :], sm2[:, b % 2, c, :], ACT.Exp,
                                         bias=nmax2[:, b, c:c + 1],
                                         accum_out=sum2[:, b, c:c + 1]).then_inc(ex2_done, 1)
            for n in range(2 * NJ):
                act.wait_ge(gu_psum, n + 1)
                if n >= 2:
                    act.wait_ge(hid_done, n - 1)
                nc.scalar.activation(sg[:, n % 2, :], psum[:, 4 + 2 * (n % 2), :], ACT.Silu).then_inc(silu_done, 1)

        @block.vector
        def _(dve):
            stt = nc.vector.scalar_tensor_tensor
            dve.wait_ge(ct_in, 16)
            nc.vector.reduce_max(cmax[:, :], ct[:, :, :].rearrange("p c n -> p (c n)"), AX_X,
                                 apply_absolute_value=True).then_inc(cmax_done, 1)
            nc.vector.memset(drive[:, T, :], 0.0).then_inc(drive_done, 1)
            dve.wait_ge(bias_in, 16)
            nc.vector.tensor_scalar(bias_d[:, :], bias_sb[:, :], -P_SHIFT, 0.5 * DT, ALU.add,
                                    ALU.mult).then_inc(bias_done, 2)
            dve.wait_ge(call_done, 1)
            nc.vector.tensor_scalar(cclip[:, :], call[:, :], 2.0 ** -100, None, ALU.max).then_inc(cprep, 1)
            dve.wait_ge(cprep, 1)
            nc.vector.tensor_scalar(cexp[:, :].bitcast(U32), cclip[:, :].bitcast(U32), EXPONENT, None,
                                    ALU.bitwise_and).then_inc(cprep, 1)
            nc.vector.tensor_scalar(cinv[:, :].bitcast(U32), cclip[:, :].bitcast(U32), EXPONENT, EXPONENT,
                                    ALU.bitwise_and, ALU.bitwise_xor).then_inc(cprep, 1)
            dve.wait_ge(cprep, 3)
            nc.vector.tensor_scalar(cscaled[:, :, :], ct[:, :, :], cinv[:, 0:1], 2.0 ** 12, ALU.mult,
                                    ALU.mult).then_inc(cprep, 1)
            for s in range(4):
                last = nc.vector.tensor_scalar(gain[:, s:s + 1], cexp[:, :], STEP[s] * 2.0 ** -13, None, ALU.mult)
                last.then_inc(gain_done, 1)
            dve.wait_ge(cprep, 4)
            nc.vector.tensor_copy(c_hi[:, :, :], cscaled[:, :, :]).then_inc(cprep, 1)
            dve.wait_ge(cprep, 5)
            nc.vector.tensor_tensor(c_lo[:, :, :], cscaled[:, :, :], c_hi[:, :, :],
                                    ALU.subtract).then_inc(c_split, 1)
            dve.wait_ge(cond_in, 16)
            nc.vector.tensor_scalar(p1[:, :], cf[:, :], -P_SHIFT, None, ALU.add)\
                .then_inc(pu_ready, 1)
            nc.vector.tensor_copy(qc[:, :], cf[:, :]).then_inc(clip_ready, 1)
            nc.vector.tensor_copy(q[:, 0, :], cf[:, :]).then_inc(q_ready[0], 1)
            dve.wait_ge(drive_done, 3)
            dve.wait_ge(clip_ready, 1)
            nc.vector.tensor_tensor(bq[:, :], qc[:, :], drive[:, 0, :], ALU.add).then_inc(linear_ready[0], 1)
            dve.wait_ge(gain_done, 4)

            def split_tanh(s, t):
                dve.wait_ge(tanh_ready[s], t + 1)
                nc.vector.tensor_tensor(th_lo[:, :], th[:, :], th_hi[:, :], ALU.subtract).then_inc(lo_ready[s], 1)

            def cubic(s, t):
                dve.wait_ge(square_ready[s], t + 1)
                stt(out=u[:, s, :], in0=sq[:, s, :], scalar=LINEAR[s], in1=(qc[:, :] if s == 0 else q[:, s, :]),
                    op0=ALU.subtract, op1=ALU.mult).then_inc(cubic_ready[s], 1)

            def add_coupling(s, t):
                dve.wait_ge(base_ready[s], t + 1)
                dve.wait_ge(coupled[s], t + 1)
                stt(out=q[:, (s + 1) % 4, :].rearrange("p (c b) -> p c b", c=NC), in0=psum[:, 0:NC, 0:B],
                    scalar=gain[:, s:s + 1], in1=base[:, s, :].rearrange("p (c b) -> p c b", c=NC),
                    op0=ALU.mult, op1=ALU.add).then_inc(q_ready[(s + 1) % 4], 1)

            with dve.Fori(0, T) as t:
                split_tanh(0, t)
                dve.wait_ge(linear_ready[0], t + 1)
                stt(out=g[:, 0, :], in0=p1[:, :], scalar=-0.5 * DT, in1=bq[:, :], op0=ALU.mult, op1=ALU.add)
                cubic(0, t)
                stt(out=y[:, 0, :], in0=p1[:, :], scalar=-BETA, in1=qc[:, :], op0=ALU.mult, op1=ALU.add)
                dve.wait_ge(cubic_ready[0], t + 1)
                nc.vector.tensor_tensor(base[:, 0, :], g[:, 0, :], u[:, 0, :], ALU.subtract)\
                    .then_inc(base_ready[0], 1)
                add_coupling(0, t)
                stt(out=r3[:, :], in0=bq[:, :], scalar=2.0, in1=qc[:, :], op0=ALU.mult, op1=ALU.subtract)
                stt(out=v1[:, :], in0=qc[:, :], scalar=-2.0, in1=bq[:, :], op0=ALU.mult, op1=ALU.add)
                stt(out=p2[:, :], in0=y[:, 0, :], scalar=E2, in1=p1[:, :], op0=ALU.mult, op1=ALU.add)
                stt(out=g[:, 1, :], in0=y[:, 0, :], scalar=-0.5 * DT * E2, in1=g[:, 0, :], op0=ALU.mult,
                    op1=ALU.add).then_inc(linear_ready[1], 1)
                split_tanh(1, t)
                dve.wait_ge(linear_ready[1], t + 1)
                stt(out=y[:, 1, :], in0=p2[:, :], scalar=-BETA, in1=q[:, 1, :], op0=ALU.mult, op1=ALU.add)
                cubic(1, t)
                nc.vector.tensor_tensor(v2[:, :], v1[:, :], q[:, 1, :], ALU.add)
                dve.wait_ge(cubic_ready[1], t + 1)
                nc.vector.tensor_tensor(base[:, 1, :], g[:, 1, :], u[:, 1, :], ALU.subtract)\
                    .then_inc(base_ready[1], 1)
                add_coupling(1, t)
                stt(out=p3[:, :], in0=y[:, 1, :], scalar=E2, in1=p1[:, :], op0=ALU.mult,
                    op1=ALU.add).then_inc(p_ready[2], 1)
                stt(out=s1[:, :], in0=y[:, 1, :], scalar=2.0, in1=y[:, 0, :], op0=ALU.mult, op1=ALU.add)
                dve.wait_ge(p_ready[2], t + 1)
                stt(out=g[:, 2, :], in0=p3[:, :], scalar=-DT, in1=r3[:, :], op0=ALU.mult,
                    op1=ALU.add).then_inc(linear_ready[2], 1)
                split_tanh(2, t)
                dve.wait_ge(linear_ready[2], t + 1)
                stt(out=y[:, 2, :], in0=p3[:, :], scalar=-BETA, in1=q[:, 2, :], op0=ALU.mult, op1=ALU.add)
                cubic(2, t)
                stt(out=v3[:, :], in0=q[:, 2, :], scalar=2.0, in1=v2[:, :], op0=ALU.mult, op1=ALU.add)
                dve.wait_ge(cubic_ready[2], t + 1)
                nc.vector.tensor_tensor(base[:, 2, :], g[:, 2, :], u[:, 2, :], ALU.subtract)\
                    .then_inc(base_ready[2], 1)
                add_coupling(2, t)
                stt(out=s2[:, :], in0=y[:, 2, :], scalar=2.0, in1=s1[:, :], op0=ALU.mult, op1=ALU.add)
                stt(out=p4[:, :], in0=y[:, 2, :], scalar=2.0 * E2, in1=p1[:, :], op0=ALU.mult,
                    op1=ALU.add).then_inc(p_ready[3], 1)
                dve.wait_ge(p_ready[3], t + 1)
                stt(out=g[:, 3, :], in0=p4[:, :], scalar=-0.5 * DT, in1=v3[:, :], op0=ALU.mult, op1=ALU.add)
                stt(out=ps_[:, :], in0=s2[:, :], scalar=DT * EPS_P / 6.0, in1=p1[:, :], op0=ALU.mult,
                    op1=ALU.add).then_inc(linear_ready[3], 1)
                split_tanh(3, t)
                dve.wait_ge(linear_ready[3], t + 1)
                stt(out=y[:, 3, :], in0=p4[:, :], scalar=-BETA, in1=q[:, 3, :], op0=ALU.mult, op1=ALU.add)
                cubic(3, t)
                dve.wait_ge(cubic_ready[3], t + 1)
                stt(out=base[:, 3, :], in0=g[:, 3, :], scalar=1.0 / 3.0, in1=u[:, 3, :], op0=ALU.mult,
                    op1=ALU.subtract).then_inc(base_ready[3], 1)
                add_coupling(3, t)
                stt(out=pu[:, :], in0=y[:, 3, :], scalar=DT * EPS_P / 6.0, in1=ps_[:, :], op0=ALU.mult,
                    op1=ALU.add).then_inc(pu_ready, 1)
                dve.wait_ge(q_ready[0], t + 2)
                dve.wait_ge(saved, t + 1)
                nc.vector.tensor_scalar(qc[:, :], q[:, 0, :], -CLAMP, CLAMP, ALU.max,
                                        ALU.min).then_inc(clip_ready, 1)
                dve.wait_ge(pu_ready, t + 2)
                nc.vector.tensor_scalar(p1[:, :], pu[:, :], -CLAMP - P_SHIFT, CLAMP - P_SHIFT, ALU.max, ALU.min)
                dve.wait_ge(clip_ready, t + 2)
                nc.vector.tensor_tensor(bq[:, :], qc[:, :],
                                        drive[:, bass.ds(t + 1, 1), :].rearrange("p a c -> p (a c)"),
                                        ALU.add).then_inc(linear_ready[0], 1)

            dve.wait_ge(folded, 1)
            nc.vector.tensor_copy(wqk[:, :, :].rearrange("p c n -> p (c n)"), psum[:, 4, :]).then_inc(folded_out, 1)
            nc.vector.tensor_copy(wvo[:, :, :].rearrange("p c n -> p (c n)"), psum[:, 5, :]).then_inc(folded_out, 1)
            nc.vector.tensor_scalar(a2[:, :], psum[:, 6, 0:P], DK ** -0.5, None, ALU.mult)
            nc.vector.tensor_copy(wvo2[:, :], psum[:, 6, P:2 * P]).then_inc(folded_out, 1)
            for b in range(B):
                dve.wait_ge(tq_copied, b // 2 + 1)
                nc.vector.bn_stats(stats[:, b, :], qtok[:, b, :]).then_inc(stats_done, 1)
            for b in range(B):
                dve.wait_ge(stats_done, b + 1)
                nc.vector.bn_aggr(mv[:, b, :], stats[:, b, :]).then_inc(mv_done, 1)
            dve.wait_ge(mv_done, B)
            nc.vector.tensor_scalar(vare[:, :], mv[:, :, 1], LN_EPS, None, ALU.add).then_inc(var_done, 1)
            dve.wait_ge(std_done, 1)
            nc.vector.reciprocal(rstd[:, :], std[:, :]).then_inc(rstd_done, 1)
            dve.wait_ge(rstd_done, 1)
            for b in range(B):
                nc.vector.tensor_scalar(xn[:, b, :], qtok[:, b, :], mv[:, b, 0:1], rstd[:, b:b + 1],
                                        ALU.subtract, ALU.mult).then_inc(xn_done, 1)
            dve.wait_ge(attn_in, 16 * 6)
            for i in range(2):
                dve.wait_ge(xnt_psum, i + 1)
                nc.vector.tensor_scalar(xnt[:, 0, i * HALF:(i + 1) * HALF], psum[:, 4 + i, :], gam[:, 0:1],
                                        bet[:, 0:1], ALU.mult, ALU.add).then_inc(xnt_dve, 1)
            for i in range(2):
                dve.wait_ge(z_psum, 2 * i + 1)
                nc.vector.tensor_copy(z[:, 0, i * HALF:(i + 1) * HALF], psum[:, i, :]).then_inc(z_dve, 1)
            for i in range(2):
                dve.wait_ge(vo_psum, 2 * i + 1)
                nc.vector.tensor_copy(vo[:, 4 * i:4 * i + 2, :].rearrange("p a n -> p (a n)"),
                                      psum[:, 4 + 2 * i, :]).then_inc(vo_dve, 1)
            dve.wait_ge(consts, 2)
            for i in range(2):
                dve.wait_ge(s_psum, i + 1)
                stt(out=sm[:, 4 * i:4 * i + 4, :], in0=psum[:, i, :].rearrange("p (a n) -> p a n", a=4),
                    scalar=float(N) ** -0.5, in1=causal[:, None, :].to_broadcast([P, 4, T]), op0=ALU.mult,
                    op1=ALU.add).then_inc(sm_done, 1)
                dve.wait_ge(sm_done, i + 1)
                nc.vector.tensor_reduce(nmax[:, 4 * i:4 * i + 4], sm[:, 4 * i:4 * i + 4, :], AX_X, ALU.max,
                                        negate=True).then_inc(nmax_done, 1)
            dve.wait_ge(ex_done, B)
            nc.vector.reciprocal(rinv[:, :], rsum[:, :]).then_inc(rinv_done, 1)
            dve.wait_ge(ext_psum, 1)
            nc.vector.tensor_copy(ext[:, 0:4, :].rearrange("p a n -> p (a n)"), psum[:, 2, :]).then_inc(ext_dve, 1)
            dve.wait_ge(rinv_done, 1)
            dve.wait_ge(resid_done, 4)
            for b in range(B):
                dve.wait_ge(o_psum, b // 2 + 1)
                stt(out=x1[:, b, :], in0=psum[:, 4 + b // 2, (b % 2) * N:(b % 2 + 1) * N], scalar=rinv[:, b:b + 1],
                    in1=resid[:, b, :], op0=ALU.mult, op1=ALU.add).then_inc(x1_done, 1)
            dve.wait_ge(hm_in, 16)
            for b in range(B):
                dve.wait_ge(x1_done, b + 1)
                nc.vector.tensor_tensor(x1h[:, b, :], x1[:, b, :], hm[:, b, :], ALU.mult).then_inc(x1h_done, 1)

            dve.wait_ge(km_done, 2)

            def masked_max(b):
                dve.wait_ge(s2_psum, b + 1)
                if b >= 2:
                    dve.wait_ge(ex2_done, 2 * (b - 1))
                for c in range(NC):
                    nc.vector.tensor_tensor_reduce(out=sm2[:, b % 2, c, :], in0=psum[:, b % 2, c * N:(c + 1) * N],
                                                   in1=km[:, b, :], scale=1.0, scalar=MASKED, op0=ALU.add,
                                                   op1=ALU.max, accum_out=max2[:, b, c:c + 1]).then_inc(sm2_done, 1)
                dve.wait_ge(sm2_done, 2 * (b + 1))
                nc.vector.tensor_scalar(nmax2[:, b, :], max2[:, b, :], -1.0, None, ALU.mult).then_inc(nmax2_done, 1)

            def turned(b):
                dve.wait_ge(ext2_psum, b + 1)
                nc.vector.tensor_copy(ext2[:, b % 2, :, :].rearrange("p c n -> p (c n)"),
                                      psum[:, 2, :]).then_inc(ext2_done, 1)
                nc.vector.reciprocal(inv2[:, b, :], sum2[:, b, :]).then_inc(inv2_done, 1)
                dve.wait_ge(inv2_done, b + 1)
                nc.vector.tensor_tensor(r2[:, b, :], inv2[:, b, :],
                                        cf[:, :].rearrange("p (c b) -> p b c", c=NC)[:, b, :],
                                        ALU.mult).then_inc(r2_done, 1)

            def weighed(b):
                dve.wait_ge(h_psum, b + 1)
                dve.wait_ge(r2_done, b + 1)
                nc.vector.tensor_tensor(ht[:, :, b * P:(b + 1) * P],
                                        psum[:, 3, 0:2 * P].rearrange("p (c e) -> p c e", c=NC),
                                        r2[:, b, :, None].to_broadcast([P, NC, P]), ALU.mult).then_inc(h_done, 1)

            def gated(n):
                dve.wait_ge(silu_done, n + 1)
                j, half = n % NJ, n // NJ
                nc.vector.tensor_tensor(hid[:, j, half * HALF:(half + 1) * HALF], sg[:, n % 2, :],
                                        psum[:, 5 + 2 * (n % 2), :], ALU.mult).then_inc(hid_done, 1)

            def finish(b):
                dve.wait_ge(y_psum, b // 2 + 1)
                nc.vector.tensor_tensor(yout[:, b, :], psum[:, b // 2, (b % 2) * N:(b % 2 + 1) * N],
                                        x1[:, b, :], ALU.add).then_inc(y_done, 1)

            masked_max(0)
            masked_max(1)
            for b in range(B):
                turned(b)
                if b + 2 < B:
                    masked_max(b + 2)
                weighed(b)
            for half in range(2):
                for j in range(NJ):
                    gated(half * NJ + j)
                for b in range(4 * half, 4 * half + 4):
                    finish(b)

        @block.tensor
        def _(pe):
            mm = nc.tensor.matmul
            pe.wait_ge(c_split, 1)

            def couple(m, part, th_part, start, stop):
                for k in range(NC):
                    last = mm(psum[:, m, 0:B], part[:, k, m * P:(m + 1) * P], th_part[:, k * B:(k + 1) * B],
                              start=(start and k == 0), stop=(stop and k == NC - 1))
                return last

            with pe.Fori(0, T) as t:
                for s in range(4):
                    pe.wait_ge(hi_ready[s], t + 1)
                    for m in range(NC):
                        couple(m, c_hi, th_hi, True, False)
                        couple(m, c_lo, th_hi, False, False)
                    pe.wait_ge(lo_ready[s], t + 1)
                    for m in range(NC):
                        last = couple(m, c_hi, th_lo, False, True)
                    last.then_inc(coupled[s], 1)

            pe.wait_ge(consts, 1)
            pe.wait_ge(saved, T + 1)
            pe.wait_ge(q_ready[0], T + 1)
            for b in range(B):
                for c in range(NC):
                    last = nc.tensor.transpose(psum[:, b // 2, (b % 2) * N + c * P:(b % 2) * N + (c + 1) * P],
                                               trace[:, :, c * B + b], ident[:, :])
                if b % 2:
                    last.then_inc(tq_ready, 1)
            pe.wait_ge(attn_in, 16 * 6)
            for i, (left, right) in enumerate(((wqt, wkt), (wvt, wo_sb))):
                for m in range(NC):
                    for k in range(NC):
                        last = mm(psum[:, 4 + i, m * N:(m + 1) * N], left[:, k, m * P:(m + 1) * P], right[:, k, :],
                                  start=(k == 0), stop=(k == NC - 1))
            pe.wait_ge(w2_in, 16 * (3 + HEADS))
            mm(psum[:, 6, 0:P], wq2[:, :], wk2[:, :], start=True, stop=True)
            mm(psum[:, 6, P:2 * P], wv2[:, :], wo2_sb[:, :], start=True, stop=True).then_inc(folded, 1)
            pe.wait_ge(folded_out, 3)
            for b in range(B):
                pe.wait_ge(xn_done, b + 1)
                for c in range(NC):
                    last = nc.tensor.transpose(psum[:, 4 + 2 * c + b // 4, (b % 4) * P:(b % 4 + 1) * P],
                                               xn[:, b, c * P:(c + 1) * P], ident[:, :])
                if b % 4 == 3:
                    last.then_inc(xnt_psum, 1)
            pe.wait_ge(tq_copied, 4)
            for i in range(2):
                pe.wait_ge(xnt_dve, i + 1)
                pe.wait_ge(xnt_act, i + 1)
                for m in range(NC):
                    for k in range(NC):
                        last = mm(psum[:, 2 * m + i, :], wqk[:, k, m * P:(m + 1) * P],
                                  xnt[:, k, i * HALF:(i + 1) * HALF], start=(k == 0), stop=(k == NC - 1))
                    last.then_inc(z_psum, 1)
            for b in range(B):
                for k in range(NC):
                    last = mm(psum[:, 4 + b // 2, (b % 2) * N:(b % 2 + 1) * N], xnt[:, k, b * P:(b + 1) * P],
                              wvo[:, k, :], start=(k == 0), stop=(k == NC - 1))
                if b % 2:
                    last.then_inc(vo_psum, 1)
            pe.wait_ge(z_dve, 2)
            pe.wait_ge(z_act, 2)
            for b in range(B):
                for k in range(NC):
                    last = mm(psum[:, b // 4, (b % 4) * T:(b % 4 + 1) * T], z[:, k, b * P:(b + 1) * P],
                              xnt[:, k, b * P:(b + 1) * P], start=(k == 0), stop=(k == NC - 1))
                if b % 4 == 3:
                    last.then_inc(s_psum, 1)
            for b in range(B):
                pe.wait_ge(ex_done, b + 1)
                last = nc.tensor.transpose(psum[:, 2 + b // 4, (b % 4) * T:(b % 4 + 1) * T], ex[:, b, :], ident[:, :])
                if b % 4 == 3:
                    last.then_inc(ext_psum, 1)
            pe.wait_ge(vo_dve, 2)
            pe.wait_ge(vo_act, 2)
            for b in range(B):
                if b % 4 == 0:
                    pe.wait_ge((ext_dve, ext_act)[b // 4], 1)
                last = mm(psum[:, 4 + b // 2, (b % 2) * N:(b % 2 + 1) * N], ext[:, b, :], vo[:, b, :],
                          start=True, stop=True)
                if b % 2:
                    last.then_inc(o_psum, 1)
            pe.wait_ge(sm_done, 2)
            for i in range(4):
                pe.wait_ge(x1_done, 2 * i + 2)
                mm(psum[:, i, :], a2[:, :], x1[:, 2 * i:2 * i + 2, :].rearrange("p a n -> p (a n)"),
                   start=True, stop=True).then_inc(z2_psum, 1)
            pe.wait_ge(x1_done, B)
            for b in range(B):
                for c in range(NC):
                    last = mm(psum[:, 4 + b // 2, (b % 2) * N + c * P:(b % 2) * N + (c + 1) * P],
                              x1[:, b, c * P:(c + 1) * P], wvo2[:, :], start=True, stop=True)
                if b % 2:
                    last.then_inc(vo2_psum, 1)

            def scores2(b):
                if b == 0:
                    pe.wait_ge(z2_act, 4)
                else:
                    pe.wait_ge(sm2_done, max(2 * (b - 1), 0))
                pe.wait_ge(x1h_done, b + 1)
                for c in range(NC):
                    last = mm(psum[:, b % 2, c * N:(c + 1) * N], z2[:, b, c * P:(c + 1) * P], x1h[:, b, :],
                              start=True, stop=True)
                last.then_inc(s2_psum, 1)

            def turn2(b):
                pe.wait_ge(ex2_done, 2 * b + 2)
                if b >= 1:
                    pe.wait_ge(ext2_done, b)
                for c in range(NC):
                    for k in range(NC):
                        last = nc.tensor.transpose(psum[:, 2, k * N + c * P:k * N + (c + 1) * P],
                                                   ex2[:, b % 2, c, k * P:(k + 1) * P], ident[:, :])
                last.then_inc(ext2_psum, 1)

            def weigh2(b):
                pe.wait_ge(ext2_done, b + 1)
                if b == 0:
                    pe.wait_ge(vo2_act, 4)
                else:
                    pe.wait_ge(h_done, b)
                for c in range(NC):
                    for k in range(NC):
                        last = mm(psum[:, 3, c * P:(c + 1) * P], ext2[:, b % 2, k, c * P:(c + 1) * P],
                                  vo2[:, b, k, :], start=(k == 0), stop=(k == NC - 1))
                last.then_inc(h_psum, 1)

            scores2(0)
            scores2(1)
            for b in range(B):
                turn2(b)
                if b + 2 < B:
                    scores2(b + 2)
                weigh2(b)

            pe.wait_ge(ffn_in, 32)
            pe.wait_ge(h_done, B)
            for half in range(2):
                for j in range(NJ):
                    n = half * NJ + j
                    if n >= 2:
                        pe.wait_ge(hid_done, n - 1)
                    for gu in range(2):
                        for k in range(NC):
                            last = mm(psum[:, 4 + 2 * (n % 2) + gu, :],
                                      wgu[:, k, gu * INTER + j * P:gu * INTER + (j + 1) * P],
                                      ht[:, k, half * HALF:(half + 1) * HALF],
                                      start=(k == 0), stop=(k == NC - 1))
                    last.then_inc(gu_psum, 1)
                pe.wait_ge(hid_done, NJ * (half + 1))
                for b in range(4 * half, 4 * half + 4):
                    for j in range(NJ):
                        last = mm(psum[:, b // 2, (b % 2) * N:(b % 2 + 1) * N], hid[:, j, b * P:(b + 1) * P],
                                  wd[:, j, :], start=(j == 0), stop=(j == NJ - 1))
                    if b % 2:
                        last.then_inc(y_psum, 1)


def kernel(x, cond_2048, L0_cond_coupling, L0_cond_bias, L0_attn_qkv, L0_attn_o_proj, L0_attn_gamma,
           L0_attn_beta, L0_cond2_Wq, L0_cond2_Wk, L0_cond2_Wv, L0_cond2_Wo, L0_ffn_w_gate_up, L0_ffn_w_down):
    import numpy as np
    import concourse.bacc as bacc
    from concourse.bass_utils import run_bass_kernel_spmd

    def chunks(a):
        a = np.asarray(a)
        a = a.reshape(a.shape[0] // P, P, *a.shape[1:])
        return np.ascontiguousarray(np.moveaxis(a, 0, 1))

    x = np.asarray(x)
    cond = np.asarray(cond_2048)
    qkv = np.asarray(L0_attn_qkv)
    arrays = {
        "x_feat": np.ascontiguousarray(x.reshape(B, T, NC, P).transpose(3, 1, 2, 0).reshape(P, T, COLS)),
        "x_tok": np.ascontiguousarray(x.transpose(1, 0, 2)),
        "cond_feat": np.ascontiguousarray(cond.reshape(B, NC, P).transpose(2, 1, 0).reshape(P, COLS)),
        "cond_row": np.ascontiguousarray(cond.reshape(B * N)),
        "coupling_t": chunks(np.asarray(L0_cond_coupling).T),
        "bias": chunks(L0_cond_bias),
        "wq_t": chunks(qkv[:, 0:N].T),
        "wk_t": chunks(qkv[:, N:2 * N].T),
        "wv_t": chunks(qkv[:, 2 * N:3 * N].T),
        "wo": chunks(L0_attn_o_proj),
        "gamma": chunks(L0_attn_gamma),
        "beta": chunks(L0_attn_beta),
        "wq2_t": np.ascontiguousarray(np.asarray(L0_cond2_Wq)[1].T),
        "wk2_t": np.ascontiguousarray(np.asarray(L0_cond2_Wk)[1].T),
        "wv2_t": np.ascontiguousarray(np.asarray(L0_cond2_Wv)[1].T),
        "wo2": np.ascontiguousarray(np.asarray(L0_cond2_Wo)),
        "w_gate_up_t": chunks(np.asarray(L0_ffn_w_gate_up).T),
        "w_down_t": chunks(np.asarray(L0_ffn_w_down).T),
    }
    nc = bacc.Bacc("TRN2", target_bir_lowering=False, num_devices=1)
    args = [nc.dram_tensor(f"in_{k}", a.shape, mybir.dt.from_np(a.dtype), kind="ExternalInput").ap()
            for k, a in arrays.items()]
    out = nc.dram_tensor("out_y", (B, T, N), F32, kind="ExternalOutput").ap()
    fhn_attention_ffn(nc, *args, out)
    result = run_bass_kernel_spmd(nc, [{f"in_{k}": a for k, a in arrays.items()}], core_ids=[0])
    return result.results[0]["out_y"]
```

```python
from contextlib import ExitStack

import concourse.bass as bass
from concourse import mybir

P = 128
B, T, N = 8, 128, 256
NC = N // P
COLS = NC * B
TOK = B * T
HALF = 512
INTER = 1024
NJ = INTER // P
HEADS, DK = 16, 8

DT = 0.01
EPS_P = 0.08
ALPHA, BETA, CLAMP = 0.7, 0.8, 20.0
P_SHIFT = ALPHA / BETA
E2 = 0.5 * DT * EPS_P
LN_EPS = 1e-5
NEG = -1e30
UNROLL = 8
MASKED = -3e38

STEP = [0.5 * DT, 0.5 * DT, DT, DT / 6.0]
LINEAR = [0.5 * DT, 0.5 * DT, DT, 1.0 / 3.0 + DT / 6.0]
CUBIC = [0.5 * DT / 3.0, 0.5 * DT / 3.0, DT / 3.0, DT / 18.0]

ALU = mybir.AluOpType
ACT = mybir.ActivationFunctionType
F32 = mybir.dt.float32
F16 = mybir.dt.float16
U32 = mybir.dt.uint32
AX_X = mybir.AxisListType.X
EXPONENT = 0x7F800000


def fhn_attention_ffn(nc, x_feat, x_tok, cond_feat, cond_row, coupling_t, bias, wq_t, wk_t, wv_t,
                      wo, gamma, beta, wq2_t, wk2_t, wv2_t, wo2, w_gate_up_t, w_down_t, out):
    with ExitStack() as ctx:
        def sb(name, shape, dt=F32):
            return ctx.enter_context(nc.sbuf_tensor(name, shape, dt))

        def sem(name):
            return ctx.enter_context(nc.semaphore(name))

        psum = ctx.enter_context(nc.psum_tensor("psum", [P, 8, HALF], F32))

        hid = sb("hid", [P, NJ, TOK])
        shared = hid[:, :, :].rearrange("p (a h) n -> p a (h n)", h=2)
        xf = shared[:, 0, :].rearrange("p (t c) -> p t c", c=COLS)
        qtok = shared[:, 1, :].rearrange("p (b n) -> p b n", b=B)
        xn = shared[:, 2, :].rearrange("p (b n) -> p b n", b=B)
        z = shared[:, 3, :].rearrange("p (c n) -> p c n", c=NC)
        xt = sb("xt", [P, B, N])
        cf = sb("cf", [P, COLS])
        ct = sb("ct", [P, NC, N])
        bias_sb = sb("bias_sb", [P, NC])
        wqt = sb("wqt", [P, NC, N])
        wkt = sb("wkt", [P, NC, N])
        wvt = sb("wvt", [P, NC, N])
        wo_sb = sb("wo_sb", [P, NC, N])
        gam = sb("gam", [P, NC])
        bet = sb("bet", [P, NC])
        hm = sb("hm", [P, B, N])
        wq2 = sb("wq2", [DK, P])
        wk2 = sb("wk2", [DK, P])
        wv2 = sb("wv2", [P, P])
        wo2_sb = sb("wo2_sb", [P, P])
        wgu = sb("wgu", [P, NC, 2 * INTER])
        wd = sb("wd", [P, NJ, N])

        ident = sb("ident", [P, P])
        causal = sb("causal", [P, T])

        cmax = sb("cmax", [P, 1])
        ones_row = sb("ones_row", [1, P])
        call = sb("call", [1, 1])
        cclip = sb("cclip", [1, 1])
        cpow = sb("cpow", [1, 2])
        cscale = sb("cscale", [P, 2])
        cscaled = sb("cscaled", [P, NC, N])
        c_hi = sb("c_hi", [P, NC, N], F16)
        c_lo = sb("c_lo", [P, NC, N], F16)
        gain = sb("gain", [P, 4])

        bias_d = sb("bias_d", [P, NC])
        drive = sb("drive", [P, T + 1, COLS])
        q = sb("q", [P, 4, COLS])
        qc = sb("qc", [P, COLS])
        p1 = sb("p1", [P, COLS])
        pu = sb("pu", [P, COLS])
        ps_ = sb("ps_", [P, COLS])
        p2 = sb("p2", [P, COLS])
        p3 = sb("p3", [P, COLS])
        p4 = sb("p4", [P, COLS])
        y = sb("y", [P, 4, COLS])
        g = sb("g", [P, 4, COLS])
        bq = sb("bq", [P, COLS])
        gp = sb("gp", [P, COLS])
        w = sb("w", [P, 4, COLS])
        drive_now = sb("drive_now", [P, COLS])
        r3 = sb("r3", [P, COLS])
        v1 = sb("v1", [P, COLS])
        v2 = sb("v2", [P, COLS])
        v3 = sb("v3", [P, COLS])
        s1 = sb("s1", [P, COLS])
        s2 = sb("s2", [P, COLS])
        u = sb("u", [P, 4, COLS])
        base = sb("base", [P, 4, COLS])
        th = psum[:, 2, 0:COLS]
        th_hi = sb("th_hi", [P, COLS], F16)
        th_lo = sb("th_lo", [P, COLS], F16)
        trace = sb("trace", [P, T, COLS])

        wqk = sb("wqk", [P, NC, N])
        wvo = sb("wvo", [P, NC, N])
        resid = sb("resid", [P, B, N])
        stats = sb("stats", [P, B, 6])
        mv = sb("mv", [P, B, 2])
        vare = sb("vare", [P, B])
        std = sb("std", [P, B])
        rstd = sb("rstd", [P, B])
        xnt = sb("xnt", [P, NC, TOK])
        vo = sb("vo", [P, B, N])
        sm = sb("sm", [P, B, T])
        nmax = sb("nmax", [P, B])
        ex = sb("ex", [P, B, T])
        rsum = sb("rsum", [P, B])
        rinv = sb("rinv", [P, B])
        ext = sb("ext", [P, B, T])
        x1 = sb("x1", [P, B, N])

        a2 = sb("a2", [P, P])
        wvo2 = sb("wvo2", [P, P])
        km = sb("km", [P, B, N])
        x1h = sb("x1h", [P, B, N])
        z2 = sb("z2", [P, B, N])
        vo2 = sb("vo2", [P, B, NC, P])
        sm2 = sb("sm2", [P, 2, NC, N])
        max2 = sb("max2", [P, B, NC])
        nmax2 = sb("nmax2", [P, B, NC])
        ex2 = sb("ex2", [P, 2, NC, N])
        sum2 = sb("sum2", [P, B, NC])
        inv2 = sb("inv2", [P, B, NC])
        r2 = sb("r2", [P, B, NC])
        ext2 = sb("ext2", [P, 2, NC, N])
        ht = xnt

        sg = sb("sg", [P, 2, HALF])
        yout = xt

        ct_in = sem("ct_in")
        cond_in = sem("cond_in")
        bias_in = sem("bias_in")
        xf_in = sem("xf_in")
        attn_in = sem("attn_in")
        xt_in = sem("xt_in")
        hm_in = sem("hm_in")
        w2_in = sem("w2_in")
        ffn_in = sem("ffn_in")
        zeroed = sem("zeroed")
        consts = sem("consts")
        cmax_done = sem("cmax_done")
        ones_done = sem("ones_done")
        cmax_row = sem("cmax_row")
        cpow_all = sem("cpow_all")
        cprep = sem("cprep")
        c_split = sem("c_split")
        bias_done = sem("bias_done")
        drive_done = sem("drive_done")
        gain_done = sem("gain_done")

        q_ready = [sem(f"q_ready{s}") for s in range(4)]
        clip_ready = sem("clip_ready")
        pu_ready = sem("pu_ready")
        hi_ready = [sem(f"hi_ready{s}") for s in range(4)]
        tanh_ready = [sem(f"tanh_ready{s}") for s in range(4)]
        lo_ready = [sem(f"lo_ready{s}") for s in range(4)]
        coupled = [sem(f"coupled{s}") for s in range(4)]
        w_ready = [sem(f"w_ready{s}") for s in range(4)]
        u_ready = [sem(f"u_ready{s}") for s in range(4)]
        base_ready = [sem(f"base_ready{s}") for s in range(4)]
        p_ready = [sem(f"p_ready{s}") for s in range(4)]
        gp_ready = sem("gp_ready")
        bq_ready = sem("bq_ready")
        drive_fed = sem("drive_fed")
        saved = sem("saved")

        folded = sem("folded")
        folded_out = sem("folded_out")
        km_done = sem("km_done")
        tq_ready = sem("tq_ready")
        tq_copied = sem("tq_copied")
        resid_done = sem("resid_done")
        stats_done = sem("stats_done")
        mv_done = sem("mv_done")
        var_done = sem("var_done")
        std_done = sem("std_done")
        rstd_done = sem("rstd_done")
        xn_done = sem("xn_done")
        xnt_psum = sem("xnt_psum")
        xnt_dve = sem("xnt_dve")
        xnt_act = sem("xnt_act")
        z_psum = sem("z_psum")
        z_dve = sem("z_dve")
        z_act = sem("z_act")
        vo_psum = sem("vo_psum")
        vo_dve = sem("vo_dve")
        vo_act = sem("vo_act")
        s_psum = sem("s_psum")
        sm_done = sem("sm_done")
        nmax_done = sem("nmax_done")
        ex_done = sem("ex_done")
        rinv_done = sem("rinv_done")
        ext_psum = sem("ext_psum")
        ext_dve = sem("ext_dve")
        ext_act = sem("ext_act")
        o_psum = sem("o_psum")
        x1_done = sem("x1_done")
        x1h_done = sem("x1h_done")
        z2_psum = sem("z2_psum")
        z2_dve = sem("z2_dve")
        z2_act = sem("z2_act")
        vo2_psum = sem("vo2_psum")
        vo2_dve = sem("vo2_dve")
        vo2_act = sem("vo2_act")
        s2_psum = sem("s2_psum")
        sm2_done = sem("sm2_done")
        nmax2_done = sem("nmax2_done")
        ex2_done = sem("ex2_done")
        inv2_done = sem("inv2_done")
        r2_done = sem("r2_done")
        ext2_psum = sem("ext2_psum")
        ext2_done = sem("ext2_done")
        h_psum = sem("h_psum")
        h_done = sem("h_done")
        gu_psum = sem("gu_psum")
        silu_done = sem("silu_done")
        hid_done = sem("hid_done")
        y_psum = sem("y_psum")
        y_done = sem("y_done")
        out_done = sem("out_done")

        block = ctx.enter_context(nc.Block())

        @block.sync
        def _(sp):
            sp.dma_start(ct[:, :, :], coupling_t).then_inc(ct_in, 16)
            sp.dma_start(cf[:, :], cond_feat).then_inc(cond_in, 16)
            sp.dma_start(bias_sb[:, :], bias).then_inc(bias_in, 16)
            sp.dma_start(xf[:, :, :], x_feat).then_inc(xf_in, 16)
            for dst, src in ((wqt, wq_t), (wkt, wk_t), (wvt, wv_t), (wo_sb, wo)):
                sp.dma_start(dst[:, :, :], src).then_inc(attn_in, 16)
            for dst, src in ((gam, gamma), (bet, beta)):
                sp.dma_start(dst[:, :], src).then_inc(attn_in, 16)
            sp.dma_start(wq2[:, :], wq2_t).then_inc(w2_in, 16)
            sp.dma_start(wk2[:, :], wk2_t).then_inc(w2_in, 16)
            sp.dma_start(wo2_sb[:, :], wo2).then_inc(w2_in, 16)
            for h in range(HEADS):
                sp.dma_start(wv2[h * DK:(h + 1) * DK, :], wv2_t).then_inc(w2_in, 16)
            sp.dma_start(hm[:, :, :].rearrange("p b n -> p (b n)"),
                         cond_row.partition_broadcast(P)).then_inc(hm_in, 16)
            sp.dma_start(xt[:, :, :], x_tok).then_inc(xt_in, 16)
            sp.dma_start(wgu[:, :, :], w_gate_up_t).then_inc(ffn_in, 16)
            sp.dma_start(wd[:, :, :], w_down_t).then_inc(ffn_in, 16)
            for b in range(B):
                sp.wait_ge(y_done, b + 1)
                sp.dma_start(out[b, :, :], yout[:, b, :]).then_inc(out_done, 16)
            sp.wait_ge(out_done, 16 * B)

        @block.gpsimd
        def _(pool):
            nc.gpsimd.memset(ident[:, :], 0.0).then_inc(zeroed, 1)
            nc.gpsimd.memset(causal[:, :], 0.0).then_inc(zeroed, 1)
            nc.gpsimd.memset(ones_row[:, :], 1.0).then_inc(ones_done, 1)
            pool.wait_ge(zeroed, 2)
            nc.gpsimd.affine_select(out=ident[:, :], in_=ident[:, :], compare_op=ALU.not_equal, fill=1.0,
                                    base=0, pattern=[[-1, P]], channel_multiplier=1).then_inc(consts, 1)
            nc.gpsimd.affine_select(out=causal[:, :], in_=causal[:, :], compare_op=ALU.is_ge, fill=MASKED,
                                    base=0, pattern=[[-1, T]], channel_multiplier=1).then_inc(consts, 1)
            pool.wait_ge(hm_in, 16)
            nc.gpsimd.tensor_scalar(km[:, :, :], hm[:, :, :], -1.0, 1.0, ALU.mult, ALU.add).then_inc(km_done, 1)
            pool.wait_ge(km_done, 1)
            nc.gpsimd.tensor_scalar(km[:, :, :], km[:, :, :], NEG, 1.0, ALU.mult, ALU.mult).then_inc(km_done, 1)
            pool.sem_inc(saved, 1)
            nc.gpsimd.memset(drive[:, T, :], 0.0).then_inc(drive_done, 1)
            pool.wait_ge(drive_done, 3)
            nc.gpsimd.tensor_copy(drive_now[:, :], drive[:, 0, :]).then_inc(drive_fed, 1)
            with pool.Fori(0, T) as t:
                pool.wait_ge(bq_ready, t + 1)
                nc.gpsimd.tensor_copy(drive_now[:, :], drive[:, bass.ds(t + 1, 1), :].rearrange("p a c -> p (a c)"))\
                    .then_inc(drive_fed, 1)
                pool.wait_ge(clip_ready, t + 2)
                nc.gpsimd.tensor_copy(trace[:, bass.ds(t, 1), :].rearrange("p a c -> p (a c)"),
                                      qc[:, :]).then_inc(saved, 1)
            pool.wait_ge(xt_in, 16)
            for i in range(4):
                pool.wait_ge(tq_copied, i + 1)
                nc.gpsimd.tensor_tensor(resid[:, 2 * i:2 * i + 2, :], xt[:, 2 * i:2 * i + 2, :],
                                        qtok[:, 2 * i:2 * i + 2, :], ALU.add).then_inc(resid_done, 1)

        @block.scalar
        def _(act):
            act.wait_ge(xf_in, 16)
            act.wait_ge(bias_done, 2)
            for c in range(NC):
                nc.scalar.activation(drive[:, 0:T, c * B:(c + 1) * B], xf[:, :, c * B:(c + 1) * B],
                                     ACT.Identity, bias=bias_d[:, c:c + 1],
                                     scale=0.5 * DT).then_inc(drive_done, 1)
            with act.Fori(0, T, UNROLL) as t0:
                count = [act.snap(t0 + k) for k in range(1, UNROLL + 1)]
                for now in count:
                    for s in range(4):
                        act.wait_ge(q_ready[s], now)
                        nc.scalar.activation(th_hi[:, :], q[:, s, :], ACT.Tanh).then_inc(hi_ready[s], 1)
                        nc.scalar.activation(th, q[:, s, :], ACT.Tanh).then_inc(tanh_ready[s], 1)

            for i in range(4):
                act.wait_ge(tq_ready, i + 1)
                nc.scalar.activation(qtok[:, 2 * i:2 * i + 2, :].rearrange("p a n -> p (a n)"),
                                     psum[:, i, :], ACT.Copy).then_inc(tq_copied, 1)
            act.wait_ge(var_done, 1)
            nc.scalar.activation(std[:, :], vare[:, :], ACT.Sqrt).then_inc(std_done, 1)
            act.wait_ge(attn_in, 16 * 6)
            for i in range(2):
                act.wait_ge(xnt_psum, i + 1)
                nc.scalar.activation(xnt[:, 1, i * HALF:(i + 1) * HALF], psum[:, 6 + i, :], ACT.Identity,
                                     bias=bet[:, 1:2], scale=gam[:, 1:2]).then_inc(xnt_act, 1)
            for i in range(2):
                act.wait_ge(z_psum, 2 * i + 2)
                nc.scalar.activation(z[:, 1, i * HALF:(i + 1) * HALF], psum[:, 2 + i, :],
                                     ACT.Copy).then_inc(z_act, 1)
            for i in range(2):
                act.wait_ge(vo_psum, 2 * i + 2)
                nc.scalar.activation(vo[:, 4 * i + 2:4 * i + 4, :].rearrange("p a n -> p (a n)"),
                                     psum[:, 5 + 2 * i, :], ACT.Copy).then_inc(vo_act, 1)
            for b in range(B):
                act.wait_ge(nmax_done, b // 4 + 1)
                nc.scalar.activation(ex[:, b, :], sm[:, b, :], ACT.Exp, bias=nmax[:, b:b + 1],
                                     accum_out=rsum[:, b:b + 1]).then_inc(ex_done, 1)
            act.wait_ge(ext_psum, 2)
            nc.scalar.activation(ext[:, 4:8, :].rearrange("p a n -> p (a n)"), psum[:, 3, :],
                                 ACT.Copy).then_inc(ext_act, 1)
            for i in range(4):
                act.wait_ge(z2_psum, i + 1)
                nc.scalar.activation(z2[:, 2 * i:2 * i + 2, :].rearrange("p a n -> p (a n)"),
                                     psum[:, i, :], ACT.Copy).then_inc(z2_act, 1)
            for i in range(4):
                act.wait_ge(vo2_psum, i + 1)
                nc.scalar.activation(vo2[:, 2 * i:2 * i + 2, :, :].rearrange("p a c n -> p (a c n)"),
                                     psum[:, 4 + i, :], ACT.Copy).then_inc(vo2_act, 1)
            for b in range(B):
                act.wait_ge(nmax2_done, b + 1)
                if b >= 2:
                    act.wait_ge(ext2_psum, b - 1)
                for c in range(NC):
                    nc.scalar.activation(ex2[:, b % 2, c, :], sm2[:, b % 2, c, :], ACT.Exp,
                                         bias=nmax2[:, b, c:c + 1],
                                         accum_out=sum2[:, b, c:c + 1]).then_inc(ex2_done, 1)
            for n in range(2 * NJ):
                act.wait_ge(gu_psum, n + 1)
                if n >= 2:
                    act.wait_ge(hid_done, n - 1)
                nc.scalar.activation(sg[:, n % 2, :], psum[:, 4 + 2 * (n % 2), :], ACT.Silu).then_inc(silu_done, 1)

        @block.vector
        def _(dve):
            stt = nc.vector.scalar_tensor_tensor
            dve.wait_ge(ct_in, 16)
            nc.vector.reduce_max(cmax[:, :], ct[:, :, :].rearrange("p c n -> p (c n)"), AX_X,
                                 apply_absolute_value=True).then_inc(cmax_done, 1)
            dve.wait_ge(bias_in, 16)
            nc.vector.tensor_scalar(bias_d[:, :], bias_sb[:, :], -P_SHIFT, 0.5 * DT, ALU.add,
                                    ALU.mult).then_inc(bias_done, 2)
            dve.wait_ge(cmax_row, 1)
            nc.vector.reduce_max(call[:, :], psum[0:1, 3, 0:P], AX_X).then_inc(cprep, 1)
            dve.wait_ge(cprep, 1)
            nc.vector.tensor_scalar(cclip[:, :], call[:, :], 2.0 ** -100, None, ALU.max).then_inc(cprep, 1)
            dve.wait_ge(cprep, 2)
            nc.vector.tensor_scalar(cpow[:, 0:1].bitcast(U32), cclip[:, :].bitcast(U32), EXPONENT, None,
                                    ALU.bitwise_and).then_inc(cprep, 1)
            nc.vector.tensor_scalar(cpow[:, 1:2].bitcast(U32), cclip[:, :].bitcast(U32), EXPONENT, EXPONENT,
                                    ALU.bitwise_and, ALU.bitwise_xor).then_inc(cprep, 1)
            dve.wait_ge(cpow_all, 1)
            nc.vector.tensor_copy(cscale[:, :], psum[:, 4, 0:2]).then_inc(cprep, 1)
            dve.wait_ge(cprep, 5)
            nc.vector.tensor_scalar(cscaled[:, :, :], ct[:, :, :], cscale[:, 1:2], 2.0 ** 12, ALU.mult,
                                    ALU.mult).then_inc(cprep, 1)
            for s in range(4):
                nc.vector.tensor_scalar(gain[:, s:s + 1], cscale[:, 0:1], STEP[s] * 2.0 ** -13, None,
                                        ALU.mult).then_inc(gain_done, 1)
            dve.wait_ge(cprep, 6)
            nc.vector.tensor_copy(c_hi[:, :, :], cscaled[:, :, :]).then_inc(cprep, 1)
            dve.wait_ge(cprep, 7)
            nc.vector.tensor_tensor(c_lo[:, :, :], cscaled[:, :, :], c_hi[:, :, :],
                                    ALU.subtract).then_inc(c_split, 1)
            dve.wait_ge(cond_in, 16)
            nc.vector.tensor_scalar(p1[:, :], cf[:, :], -P_SHIFT, None, ALU.add).then_inc(p_ready[0], 1)
            nc.vector.tensor_copy(qc[:, :], cf[:, :]).then_inc(clip_ready, 1)
            dve.sem_inc(pu_ready, 1)
            nc.vector.tensor_copy(q[:, 0, :], cf[:, :]).then_inc(q_ready[0], 1)
            dve.wait_ge(gain_done, 4)
            dve.wait_ge(drive_fed, 1)

            def axpy(dst, a, scalar, b, op1=ALU.add):
                return stt(out=dst, in0=a, scalar=scalar, in1=b, op0=ALU.mult, op1=op1)

            def square(s, qs):
                return stt(out=w[:, s, :], in0=qs, scalar=CUBIC[s], in1=qs, op0=ALU.mult,
                           op1=ALU.mult).then_inc(w_ready[s], 1)

            def cubic(s, qs, now):
                dve.wait_ge(w_ready[s], now)
                stt(out=u[:, s, :], in0=w[:, s, :], scalar=LINEAR[s], in1=qs, op0=ALU.subtract,
                    op1=ALU.mult).then_inc(u_ready[s], 1)

            def split_tanh(s, now):
                dve.wait_ge(tanh_ready[s], now)
                nc.vector.tensor_tensor(th_lo[:, :], th, th_hi[:, :], ALU.subtract).then_inc(lo_ready[s], 1)

            def sum_base(s, now):
                dve.wait_ge(u_ready[s], now)
                axpy(base[:, s, :], g[:, s, :], 1.0 / 3.0 if s == 3 else 1.0, u[:, s, :],
                     ALU.subtract).then_inc(base_ready[s], 1)

            def add_coupling(s, now):
                dve.wait_ge(coupled[s], now)
                stt(out=q[:, (s + 1) % 4, :].rearrange("p (c b) -> p c b", c=NC), in0=psum[:, 0:NC, 0:B],
                    scalar=gain[:, s:s + 1], in1=base[:, s, :].rearrange("p (c b) -> p c b", c=NC),
                    op0=ALU.mult, op1=ALU.add).then_inc(q_ready[(s + 1) % 4], 1)

            def stage_one_inputs(now):
                dve.wait_ge(p_ready[0], now)
                axpy(gp[:, :], p1[:, :], -0.5 * DT, drive_now[:, :]).then_inc(gp_ready, 1)
                dve.wait_ge(clip_ready, now)
                square(0, qc[:, :])
                dve.wait_ge(gp_ready, now)
                nc.vector.tensor_tensor(g[:, 0, :], gp[:, :], qc[:, :], ALU.add)

            with dve.Fori(0, T, UNROLL) as t0:
                count = [dve.snap(t0 + k) for k in range(1, UNROLL + 2)]
                for now, after in zip(count, count[1:]):
                    stage_one_inputs(now)
                    split_tanh(0, now)
                    cubic(0, qc[:, :], now)
                    axpy(y[:, 0, :], p1[:, :], -BETA, qc[:, :])
                    sum_base(0, now)
                    dve.wait_ge(base_ready[0], now)
                    nc.vector.tensor_tensor(bq[:, :], qc[:, :], drive_now[:, :], ALU.add).then_inc(bq_ready, 1)
                    add_coupling(0, now)
                    axpy(p2[:, :], y[:, 0, :], E2, p1[:, :])
                    dve.wait_ge(q_ready[1], now)
                    square(1, q[:, 1, :])
                    axpy(g[:, 1, :], y[:, 0, :], -0.5 * DT * E2, g[:, 0, :])
                    axpy(v1[:, :], qc[:, :], -2.0, bq[:, :])
                    cubic(1, q[:, 1, :], now)
                    split_tanh(1, now)
                    axpy(y[:, 1, :], p2[:, :], -BETA, q[:, 1, :])
                    sum_base(1, now)
                    axpy(r3[:, :], bq[:, :], 2.0, qc[:, :], ALU.subtract)
                    dve.wait_ge(base_ready[1], now)
                    nc.vector.tensor_tensor(v2[:, :], v1[:, :], q[:, 1, :], ALU.add)
                    add_coupling(1, now)
                    axpy(p3[:, :], y[:, 1, :], E2, p1[:, :]).then_inc(p_ready[2], 1)
                    dve.wait_ge(q_ready[2], now)
                    square(2, q[:, 2, :])
                    axpy(s1[:, :], y[:, 1, :], 2.0, y[:, 0, :])
                    dve.wait_ge(p_ready[2], now)
                    axpy(g[:, 2, :], p3[:, :], -DT, r3[:, :])
                    cubic(2, q[:, 2, :], now)
                    split_tanh(2, now)
                    dve.wait_ge(drive_fed, after)
                    axpy(y[:, 2, :], p3[:, :], -BETA, q[:, 2, :])
                    sum_base(2, now)
                    dve.wait_ge(base_ready[2], now)
                    axpy(v3[:, :], q[:, 2, :], 2.0, v2[:, :])
                    add_coupling(2, now)
                    axpy(s2[:, :], y[:, 2, :], 2.0, s1[:, :])
                    axpy(p4[:, :], y[:, 2, :], 2.0 * E2, p1[:, :]).then_inc(p_ready[3], 1)
                    dve.wait_ge(q_ready[3], now)
                    square(3, q[:, 3, :])
                    dve.wait_ge(p_ready[3], now)
                    axpy(g[:, 3, :], p4[:, :], -0.5 * DT, v3[:, :])
                    cubic(3, q[:, 3, :], now)
                    split_tanh(3, now)
                    axpy(ps_[:, :], s2[:, :], DT * EPS_P / 6.0, p1[:, :])
                    dve.wait_ge(saved, now)
                    axpy(y[:, 3, :], p4[:, :], -BETA, q[:, 3, :])
                    sum_base(3, now)
                    dve.wait_ge(base_ready[3], now)
                    axpy(pu[:, :], y[:, 3, :], DT * EPS_P / 6.0, ps_[:, :]).then_inc(pu_ready, 1)
                    add_coupling(3, now)
                    dve.wait_ge(pu_ready, after)
                    nc.vector.tensor_scalar(p1[:, :], pu[:, :], -CLAMP - P_SHIFT, CLAMP - P_SHIFT, ALU.max,
                                            ALU.min).then_inc(p_ready[0], 1)
                    dve.wait_ge(q_ready[0], after)
                    nc.vector.tensor_scalar(qc[:, :], q[:, 0, :], -CLAMP, CLAMP, ALU.max,
                                            ALU.min).then_inc(clip_ready, 1)

            dve.wait_ge(folded, 1)
            nc.vector.tensor_copy(wqk[:, :, :].rearrange("p c n -> p (c n)"), psum[:, 4, :]).then_inc(folded_out, 1)
            nc.vector.tensor_copy(wvo[:, :, :].rearrange("p c n -> p (c n)"), psum[:, 5, :]).then_inc(folded_out, 1)
            nc.vector.tensor_scalar(a2[:, :], psum[:, 6, 0:P], DK ** -0.5, None, ALU.mult)
            nc.vector.tensor_copy(wvo2[:, :], psum[:, 6, P:2 * P]).then_inc(folded_out, 1)
            for b in range(B):
                dve.wait_ge(tq_copied, b // 2 + 1)
                nc.vector.bn_stats(stats[:, b, :], qtok[:, b, :]).then_inc(stats_done, 1)
            for b in range(B):
                dve.wait_ge(stats_done, b + 1)
                nc.vector.bn_aggr(mv[:, b, :], stats[:, b, :]).then_inc(mv_done, 1)
            dve.wait_ge(mv_done, B)
            nc.vector.tensor_scalar(vare[:, :], mv[:, :, 1], LN_EPS, None, ALU.add).then_inc(var_done, 1)
            dve.wait_ge(std_done, 1)
            nc.vector.reciprocal(rstd[:, :], std[:, :]).then_inc(rstd_done, 1)
            dve.wait_ge(rstd_done, 1)
            for b in range(B):
                nc.vector.tensor_scalar(xn[:, b, :], qtok[:, b, :], mv[:, b, 0:1], rstd[:, b:b + 1],
                                        ALU.subtract, ALU.mult).then_inc(xn_done, 1)
            dve.wait_ge(attn_in, 16 * 6)
            for i in range(2):
                dve.wait_ge(xnt_psum, i + 1)
                nc.vector.tensor_scalar(xnt[:, 0, i * HALF:(i + 1) * HALF], psum[:, 4 + i, :], gam[:, 0:1],
                                        bet[:, 0:1], ALU.mult, ALU.add).then_inc(xnt_dve, 1)
            for i in range(2):
                dve.wait_ge(z_psum, 2 * i + 1)
                nc.vector.tensor_copy(z[:, 0, i * HALF:(i + 1) * HALF], psum[:, i, :]).then_inc(z_dve, 1)
            for i in range(2):
                dve.wait_ge(vo_psum, 2 * i + 1)
                nc.vector.tensor_copy(vo[:, 4 * i:4 * i + 2, :].rearrange("p a n -> p (a n)"),
                                      psum[:, 4 + 2 * i, :]).then_inc(vo_dve, 1)
            dve.wait_ge(consts, 2)
            for i in range(2):
                dve.wait_ge(s_psum, i + 1)
                stt(out=sm[:, 4 * i:4 * i + 4, :], in0=psum[:, i, :].rearrange("p (a n) -> p a n", a=4),
                    scalar=float(N) ** -0.5, in1=causal[:, None, :].to_broadcast([P, 4, T]), op0=ALU.mult,
                    op1=ALU.add).then_inc(sm_done, 1)
                dve.wait_ge(sm_done, i + 1)
                nc.vector.tensor_reduce(nmax[:, 4 * i:4 * i + 4], sm[:, 4 * i:4 * i + 4, :], AX_X, ALU.max,
                                        negate=True).then_inc(nmax_done, 1)
            dve.wait_ge(ex_done, B)
            nc.vector.reciprocal(rinv[:, :], rsum[:, :]).then_inc(rinv_done, 1)
            dve.wait_ge(ext_psum, 1)
            nc.vector.tensor_copy(ext[:, 0:4, :].rearrange("p a n -> p (a n)"), psum[:, 2, :]).then_inc(ext_dve, 1)
            dve.wait_ge(rinv_done, 1)
            dve.wait_ge(resid_done, 4)
            for b in range(B):
                dve.wait_ge(o_psum, b // 2 + 1)
                stt(out=x1[:, b, :], in0=psum[:, 4 + b // 2, (b % 2) * N:(b % 2 + 1) * N], scalar=rinv[:, b:b + 1],
                    in1=resid[:, b, :], op0=ALU.mult, op1=ALU.add).then_inc(x1_done, 1)
            dve.wait_ge(hm_in, 16)
            for b in range(B):
                dve.wait_ge(x1_done, b + 1)
                nc.vector.tensor_tensor(x1h[:, b, :], x1[:, b, :], hm[:, b, :], ALU.mult).then_inc(x1h_done, 1)

            dve.wait_ge(km_done, 2)

            def masked_max(b):
                dve.wait_ge(s2_psum, b + 1)
                if b >= 2:
                    dve.wait_ge(ex2_done, 2 * (b - 1))
                for c in range(NC):
                    nc.vector.tensor_tensor_reduce(out=sm2[:, b % 2, c, :], in0=psum[:, b % 2, c * N:(c + 1) * N],
                                                   in1=km[:, b, :], scale=1.0, scalar=MASKED, op0=ALU.add,
                                                   op1=ALU.max, accum_out=max2[:, b, c:c + 1]).then_inc(sm2_done, 1)
                dve.wait_ge(sm2_done, 2 * (b + 1))
                nc.vector.tensor_scalar(nmax2[:, b, :], max2[:, b, :], -1.0, None, ALU.mult).then_inc(nmax2_done, 1)

            def turned(b):
                dve.wait_ge(ext2_psum, b + 1)
                nc.vector.tensor_copy(ext2[:, b % 2, :, :].rearrange("p c n -> p (c n)"),
                                      psum[:, 2, :]).then_inc(ext2_done, 1)
                nc.vector.reciprocal(inv2[:, b, :], sum2[:, b, :]).then_inc(inv2_done, 1)
                dve.wait_ge(inv2_done, b + 1)
                nc.vector.tensor_tensor(r2[:, b, :], inv2[:, b, :],
                                        cf[:, :].rearrange("p (c b) -> p b c", c=NC)[:, b, :],
                                        ALU.mult).then_inc(r2_done, 1)

            def weighed(b):
                dve.wait_ge(h_psum, b + 1)
                dve.wait_ge(r2_done, b + 1)
                nc.vector.tensor_tensor(ht[:, :, b * P:(b + 1) * P],
                                        psum[:, 3, 0:2 * P].rearrange("p (c e) -> p c e", c=NC),
                                        r2[:, b, :, None].to_broadcast([P, NC, P]), ALU.mult).then_inc(h_done, 1)

            def gated(n):
                dve.wait_ge(silu_done, n + 1)
                j, half = n % NJ, n // NJ
                nc.vector.tensor_tensor(hid[:, j, half * HALF:(half + 1) * HALF], sg[:, n % 2, :],
                                        psum[:, 5 + 2 * (n % 2), :], ALU.mult).then_inc(hid_done, 1)

            def finish(b):
                dve.wait_ge(y_psum, b // 2 + 1)
                nc.vector.tensor_tensor(yout[:, b, :], psum[:, b // 2, (b % 2) * N:(b % 2 + 1) * N],
                                        x1[:, b, :], ALU.add).then_inc(y_done, 1)

            masked_max(0)
            masked_max(1)
            for b in range(B):
                turned(b)
                if b + 2 < B:
                    masked_max(b + 2)
                weighed(b)
            for half in range(2):
                for j in range(NJ):
                    gated(half * NJ + j)
                for b in range(4 * half, 4 * half + 4):
                    finish(b)

        @block.tensor
        def _(pe):
            mm = nc.tensor.matmul
            pe.wait_ge(consts, 1)
            pe.wait_ge(cmax_done, 1)
            nc.tensor.transpose(psum[0:1, 3, 0:P], cmax[:, :], ident[:, :]).then_inc(cmax_row, 1)
            pe.wait_ge(ones_done, 1)
            pe.wait_ge(cprep, 4)
            mm(psum[:, 4, 0:2], ones_row[:, :], cpow[:, :], start=True, stop=True).then_inc(cpow_all, 1)
            pe.wait_ge(c_split, 1)

            def couple(m, part, th_part, start, stop):
                for k in range(NC):
                    last = mm(psum[:, m, 0:B], part[:, k, m * P:(m + 1) * P], th_part[:, k * B:(k + 1) * B],
                              start=(start and k == 0), stop=(stop and k == NC - 1))
                return last

            with pe.Fori(0, T, UNROLL) as t0:
                count = [pe.snap(t0 + k) for k in range(1, UNROLL + 1)]
                for now in count:
                    for s in range(4):
                        pe.wait_ge(hi_ready[s], now)
                        for m in range(NC):
                            couple(m, c_hi, th_hi, True, False)
                            couple(m, c_lo, th_hi, False, False)
                        pe.wait_ge(lo_ready[s], now)
                        for m in range(NC):
                            last = couple(m, c_hi, th_lo, False, True)
                        last.then_inc(coupled[s], 1)

            pe.wait_ge(consts, 1)
            pe.wait_ge(saved, T + 1)
            pe.wait_ge(q_ready[0], T + 1)
            for b in range(B):
                for c in range(NC):
                    last = nc.tensor.transpose(psum[:, b // 2, (b % 2) * N + c * P:(b % 2) * N + (c + 1) * P],
                                               trace[:, :, c * B + b], ident[:, :])
                if b % 2:
                    last.then_inc(tq_ready, 1)
            pe.wait_ge(attn_in, 16 * 6)
            for i, (left, right) in enumerate(((wqt, wkt), (wvt, wo_sb))):
                for m in range(NC):
                    for k in range(NC):
                        last = mm(psum[:, 4 + i, m * N:(m + 1) * N], left[:, k, m * P:(m + 1) * P], right[:, k, :],
                                  start=(k == 0), stop=(k == NC - 1))
            pe.wait_ge(w2_in, 16 * (3 + HEADS))
            mm(psum[:, 6, 0:P], wq2[:, :], wk2[:, :], start=True, stop=True)
            mm(psum[:, 6, P:2 * P], wv2[:, :], wo2_sb[:, :], start=True, stop=True).then_inc(folded, 1)
            pe.wait_ge(folded_out, 3)
            for b in range(B):
                pe.wait_ge(xn_done, b + 1)
                for c in range(NC):
                    last = nc.tensor.transpose(psum[:, 4 + 2 * c + b // 4, (b % 4) * P:(b % 4 + 1) * P],
                                               xn[:, b, c * P:(c + 1) * P], ident[:, :])
                if b % 4 == 3:
                    last.then_inc(xnt_psum, 1)
            pe.wait_ge(tq_copied, 4)
            for i in range(2):
                pe.wait_ge(xnt_dve, i + 1)
                pe.wait_ge(xnt_act, i + 1)
                for m in range(NC):
                    for k in range(NC):
                        last = mm(psum[:, 2 * m + i, :], wqk[:, k, m * P:(m + 1) * P],
                                  xnt[:, k, i * HALF:(i + 1) * HALF], start=(k == 0), stop=(k == NC - 1))
                    last.then_inc(z_psum, 1)
            for b in range(B):
                for k in range(NC):
                    last = mm(psum[:, 4 + b // 2, (b % 2) * N:(b % 2 + 1) * N], xnt[:, k, b * P:(b + 1) * P],
                              wvo[:, k, :], start=(k == 0), stop=(k == NC - 1))
                if b % 2:
                    last.then_inc(vo_psum, 1)
            pe.wait_ge(z_dve, 2)
            pe.wait_ge(z_act, 2)
            for b in range(B):
                for k in range(NC):
                    last = mm(psum[:, b // 4, (b % 4) * T:(b % 4 + 1) * T], z[:, k, b * P:(b + 1) * P],
                              xnt[:, k, b * P:(b + 1) * P], start=(k == 0), stop=(k == NC - 1))
                if b % 4 == 3:
                    last.then_inc(s_psum, 1)
            for b in range(B):
                pe.wait_ge(ex_done, b + 1)
                last = nc.tensor.transpose(psum[:, 2 + b // 4, (b % 4) * T:(b % 4 + 1) * T], ex[:, b, :], ident[:, :])
                if b % 4 == 3:
                    last.then_inc(ext_psum, 1)
            pe.wait_ge(vo_dve, 2)
            pe.wait_ge(vo_act, 2)
            for b in range(B):
                if b % 4 == 0:
                    pe.wait_ge((ext_dve, ext_act)[b // 4], 1)
                last = mm(psum[:, 4 + b // 2, (b % 2) * N:(b % 2 + 1) * N], ext[:, b, :], vo[:, b, :],
                          start=True, stop=True)
                if b % 2:
                    last.then_inc(o_psum, 1)
            pe.wait_ge(sm_done, 2)
            for i in range(4):
                pe.wait_ge(x1_done, 2 * i + 2)
                mm(psum[:, i, :], a2[:, :], x1[:, 2 * i:2 * i + 2, :].rearrange("p a n -> p (a n)"),
                   start=True, stop=True).then_inc(z2_psum, 1)
            pe.wait_ge(x1_done, B)
            for b in range(B):
                for c in range(NC):
                    last = mm(psum[:, 4 + b // 2, (b % 2) * N + c * P:(b % 2) * N + (c + 1) * P],
                              x1[:, b, c * P:(c + 1) * P], wvo2[:, :], start=True, stop=True)
                if b % 2:
                    last.then_inc(vo2_psum, 1)

            def scores2(b):
                if b == 0:
                    pe.wait_ge(z2_act, 4)
                else:
                    pe.wait_ge(sm2_done, max(2 * (b - 1), 0))
                pe.wait_ge(x1h_done, b + 1)
                for c in range(NC):
                    last = mm(psum[:, b % 2, c * N:(c + 1) * N], z2[:, b, c * P:(c + 1) * P], x1h[:, b, :],
                              start=True, stop=True)
                last.then_inc(s2_psum, 1)

            def turn2(b):
                pe.wait_ge(ex2_done, 2 * b + 2)
                if b >= 1:
                    pe.wait_ge(ext2_done, b)
                for c in range(NC):
                    for k in range(NC):
                        last = nc.tensor.transpose(psum[:, 2, k * N + c * P:k * N + (c + 1) * P],
                                                   ex2[:, b % 2, c, k * P:(k + 1) * P], ident[:, :])
                last.then_inc(ext2_psum, 1)

            def weigh2(b):
                pe.wait_ge(ext2_done, b + 1)
                if b == 0:
                    pe.wait_ge(vo2_act, 4)
                else:
                    pe.wait_ge(h_done, b)
                for c in range(NC):
                    for k in range(NC):
                        last = mm(psum[:, 3, c * P:(c + 1) * P], ext2[:, b % 2, k, c * P:(c + 1) * P],
                                  vo2[:, b, k, :], start=(k == 0), stop=(k == NC - 1))
                last.then_inc(h_psum, 1)

            scores2(0)
            scores2(1)
            for b in range(B):
                turn2(b)
                if b + 2 < B:
                    scores2(b + 2)
                weigh2(b)

            pe.wait_ge(ffn_in, 32)
            pe.wait_ge(h_done, B)
            for half in range(2):
                for j in range(NJ):
                    n = half * NJ + j
                    if n >= 2:
                        pe.wait_ge(hid_done, n - 1)
                    for gu in range(2):
                        for k in range(NC):
                            last = mm(psum[:, 4 + 2 * (n % 2) + gu, :],
                                      wgu[:, k, gu * INTER + j * P:gu * INTER + (j + 1) * P],
                                      ht[:, k, half * HALF:(half + 1) * HALF],
                                      start=(k == 0), stop=(k == NC - 1))
                    last.then_inc(gu_psum, 1)
                pe.wait_ge(hid_done, NJ * (half + 1))
                for b in range(4 * half, 4 * half + 4):
                    for j in range(NJ):
                        last = mm(psum[:, b // 2, (b % 2) * N:(b % 2 + 1) * N], hid[:, j, b * P:(b + 1) * P],
                                  wd[:, j, :], start=(j == 0), stop=(j == NJ - 1))
                    if b % 2:
                        last.then_inc(y_psum, 1)


def kernel(x, cond_2048, L0_cond_coupling, L0_cond_bias, L0_attn_qkv, L0_attn_o_proj, L0_attn_gamma,
           L0_attn_beta, L0_cond2_Wq, L0_cond2_Wk, L0_cond2_Wv, L0_cond2_Wo, L0_ffn_w_gate_up, L0_ffn_w_down):
    import numpy as np
    import concourse.bacc as bacc
    from concourse.bass_utils import run_bass_kernel_spmd

    def chunks(a):
        a = np.asarray(a)
        a = a.reshape(a.shape[0] // P, P, *a.shape[1:])
        return np.ascontiguousarray(np.moveaxis(a, 0, 1))

    x = np.asarray(x)
    cond = np.asarray(cond_2048)
    qkv = np.asarray(L0_attn_qkv)
    arrays = {
        "x_feat": np.ascontiguousarray(x.reshape(B, T, NC, P).transpose(3, 1, 2, 0).reshape(P, T, COLS)),
        "x_tok": np.ascontiguousarray(x.transpose(1, 0, 2)),
        "cond_feat": np.ascontiguousarray(cond.reshape(B, NC, P).transpose(2, 1, 0).reshape(P, COLS)),
        "cond_row": np.ascontiguousarray(cond.reshape(B * N)),
        "coupling_t": chunks(np.asarray(L0_cond_coupling).T),
        "bias": chunks(L0_cond_bias),
        "wq_t": chunks(qkv[:, 0:N].T),
        "wk_t": chunks(qkv[:, N:2 * N].T),
        "wv_t": chunks(qkv[:, 2 * N:3 * N].T),
        "wo": chunks(L0_attn_o_proj),
        "gamma": chunks(L0_attn_gamma),
        "beta": chunks(L0_attn_beta),
        "wq2_t": np.ascontiguousarray(np.asarray(L0_cond2_Wq)[1].T),
        "wk2_t": np.ascontiguousarray(np.asarray(L0_cond2_Wk)[1].T),
        "wv2_t": np.ascontiguousarray(np.asarray(L0_cond2_Wv)[1].T),
        "wo2": np.ascontiguousarray(np.asarray(L0_cond2_Wo)),
        "w_gate_up_t": chunks(np.asarray(L0_ffn_w_gate_up).T),
        "w_down_t": chunks(np.asarray(L0_ffn_w_down).T),
    }
    nc = bacc.Bacc("TRN2", target_bir_lowering=False, num_devices=1)
    args = [nc.dram_tensor(f"in_{k}", a.shape, mybir.dt.from_np(a.dtype), kind="ExternalInput").ap()
            for k, a in arrays.items()]
    out = nc.dram_tensor("out_y", (B, T, N), F32, kind="ExternalOutput").ap()
    fhn_attention_ffn(nc, *args, out)
    result = run_bass_kernel_spmd(nc, [{f"in_{k}": a for k, a in arrays.items()}], core_ids=[0])
    return result.results[0]["out_y"]
```

```python
from contextlib import ExitStack

import concourse.bass as bass
from concourse import mybir

P = 128
B, T, N = 8, 128, 256
NC = N // P
COLS = NC * B
TOK = B * T
HALF = 512
INTER = 1024
NJ = INTER // P
HEADS, DK = 16, 8

DT = 0.01
EPS_P = 0.08
ALPHA, BETA, CLAMP = 0.7, 0.8, 20.0
P_SHIFT = ALPHA / BETA
E2 = 0.5 * DT * EPS_P
LN_EPS = 1e-5
NEG = -1e30
MASKED = -3e38
UNROLL = 16
GATE_UP_COLS = NC * 2 * INTER
W_COLS = GATE_UP_COLS + NJ * N
SPLIT_STEPS = 96
SPLIT_COLS = W_COLS // SPLIT_STEPS

STEP = [0.5 * DT, 0.5 * DT, DT, DT / 6.0]
LINEAR = [1.0 + 0.5 * DT, 0.5 * DT, DT, 1.0 / 3.0 + DT / 6.0]
CUBIC = [0.5 * DT / 3.0, 0.5 * DT / 3.0, DT / 3.0, DT / 18.0]

ALU = mybir.AluOpType
ACT = mybir.ActivationFunctionType
F32 = mybir.dt.float32
F16 = mybir.dt.float16
F32R = mybir.dt.float32r
U32 = mybir.dt.uint32
AX_X = mybir.AxisListType.X
EXPONENT = 0x7F800000


def fhn_attention_ffn(nc, x_feat, x_tok, cond_feat, cond_row, coupling_t, bias, wq_t, wk_t, wv_t,
                      wo, gamma, beta, wq2_t, wk2_t, wv2_t, wo2, w_gate_up_t, w_down_t, out):
    with ExitStack() as ctx:
        def sb(name, shape, dt=F32):
            return ctx.enter_context(nc.sbuf_tensor(name, shape, dt))

        def sem(name):
            return ctx.enter_context(nc.semaphore(name))

        psum = ctx.enter_context(nc.psum_tensor("psum", [P, 8, HALF], F32))

        qtok = sb("qtok", [P, B, N])
        xf = qtok[:, :, :].rearrange("p b n -> p (b n)").rearrange("p (t c) -> p t c", c=COLS)
        xt = sb("xt", [P, B, N])
        cf = sb("cf", [P, COLS])
        ct = sb("ct", [P, NC, N])
        bias_sb = sb("bias_sb", [P, NC])
        wqt = sb("wqt", [P, NC, N])
        wkt = sb("wkt", [P, NC, N])
        wvt = sb("wvt", [P, NC, N])
        wo_sb = sb("wo_sb", [P, NC, N])
        gam = sb("gam", [P, NC])
        bet = sb("bet", [P, NC])
        hm = sb("hm", [P, B, N])
        wq2 = sb("wq2", [DK, P])
        wk2 = sb("wk2", [DK, P])
        wv2 = sb("wv2", [P, P])
        wo2_sb = sb("wo2_sb", [P, P])
        w_ffn = sb("w_ffn", [P, W_COLS])
        w_hi = sb("w_hi", [P, W_COLS], F32R)
        w_lo = sb("w_lo", [P, W_COLS], F32R)

        ident = sb("ident", [P, P])
        causal = sb("causal", [P, T])

        cmax = sb("cmax", [P, 1])
        ones_row = sb("ones_row", [1, P])
        call = sb("call", [1, 1])
        cclip = sb("cclip", [1, 1])
        cpow = sb("cpow", [1, 2])
        cscale = sb("cscale", [P, 2])
        cscaled = sb("cscaled", [P, NC, N])
        c_hi = sb("c_hi", [P, NC, N], F16)
        c_lo = sb("c_lo", [P, NC, N], F16)
        gain = sb("gain", [P, 4])

        bias_d = sb("bias_d", [P, NC])
        drive = sb("drive", [P, T + 1, COLS])
        q = sb("q", [P, 4, COLS])
        q1 = sb("q1", [P, COLS])
        p1 = sb("p1", [P, COLS])
        p_sum1, p_sum2, p_sum3, p_next = [sb(n, [P, COLS]) for n in ("p_sum1", "p_sum2", "p_sum3", "p_next")]
        p2 = sb("p2", [P, COLS])
        p3 = sb("p3", [P, COLS])
        p4 = sb("p4", [P, COLS])
        rate = sb("rate", [P, 4, COLS])
        affine = sb("affine", [P, 4, COLS])
        drive_less_p = sb("drive_less_p", [P, COLS])
        square = sb("square", [P, 4, COLS])
        q_drive = sb("q_drive", [P, COLS])
        drive_now = sb("drive_now", [P, COLS])
        q_2drive = sb("q_2drive", [P, COLS])
        q_sum1 = sb("q_sum1", [P, COLS])
        q_sum2 = sb("q_sum2", [P, COLS])
        q_sum3 = sb("q_sum3", [P, COLS])
        poly = sb("poly", [P, 4, COLS])
        base = sb("base", [P, 4, COLS])
        th = psum[:, 2, 0:COLS]
        q_act = psum[:, 3, 0:COLS]
        coupling_sum = psum[:, :, :].rearrange("p (s b) n -> p s b n", s=2)
        th_hi = sb("th_hi", [P, COLS], F16)
        th_lo = sb("th_lo", [P, COLS], F16)
        trace = sb("trace", [P, T, COLS])
        xn = drive[:, 0:T, :].rearrange("p t c -> p (t c)").rearrange("p (b n) -> p b n", b=B)
        z = trace[:, :, :].rearrange("p t c -> p (t c)").rearrange("p (c n) -> p c n", c=NC)

        wqk = sb("wqk", [P, NC, N])
        wvo = sb("wvo", [P, NC, N])
        resid = sb("resid", [P, B, N])
        stats = sb("stats", [P, B, 6])
        mv = sb("mv", [P, B, 2])
        vare = sb("vare", [P, B])
        std = sb("std", [P, B])
        sqrt_first = sb("sqrt_first", [P, 1])
        rstd = sb("rstd", [P, B])
        xnt, vo, x1 = [w_ffn[:, i * NC * TOK:(i + 1) * NC * TOK] for i in range(3)]
        xnt = xnt.rearrange("p (c n) -> p c n", c=NC)
        vo = vo.rearrange("p (b n) -> p b n", b=B)
        x1 = x1.rearrange("p (b n) -> p b n", b=B)
        sm = sb("sm", [P, B, T])
        nmax = sb("nmax", [P, B])
        ex = sb("ex", [P, B, T])
        rsum = sb("rsum", [P, B])
        rinv = sb("rinv", [P, B])
        ext = sb("ext", [P, B, T])

        a2 = sb("a2", [P, P])
        wvo2 = sb("wvo2", [P, P])
        km = sb("km", [P, B, N])
        x1h = resid
        z2 = xnt.rearrange("p c n -> p (c n)").rearrange("p (b n) -> p b n", b=B)
        vo2 = vo.rearrange("p b (c e) -> p b c e", c=NC)
        sm2 = sm[:, :, :].rearrange("p b t -> p (b t)").rearrange("p (i c n) -> p i c n", i=2, c=NC)
        max2 = sb("max2", [P, B, NC])
        nmax2 = sb("nmax2", [P, B, NC])
        ex2 = ex[:, :, :].rearrange("p b t -> p (b t)").rearrange("p (i c n) -> p i c n", i=2, c=NC)
        sum2 = sb("sum2", [P, B, NC])
        inv2 = sb("inv2", [P, B, NC])
        r2 = sb("r2", [P, B, NC])
        ext2 = sb("ext2", [P, 2, NC, N])

        ht_hi = sb("ht_hi", [P, NC, TOK], F32R)
        ht_lo = sb("ht_lo", [P, NC, TOK], F32R)
        hid_hi = sb("hid_hi", [P, 3, HALF], F32R)
        hid_lo = sb("hid_lo", [P, 3, HALF], F32R)
        gate_up = [part[:, 0:GATE_UP_COLS].rearrange("p (k o) -> p k o", k=NC) for part in (w_hi, w_lo)]
        down = [part[:, GATE_UP_COLS:W_COLS].rearrange("p (j n) -> p j n", j=NJ) for part in (w_hi, w_lo)]
        sg = sm[:, :, :].rearrange("p b t -> p (b t)").rearrange("p (i n) -> p i n", n=HALF)
        hid = ex[:, :, :].rearrange("p b t -> p (b t)").rearrange("p (i n) -> p i n", n=HALF)
        yout = xt

        ct_in = sem("ct_in")
        cond_in = sem("cond_in")
        bias_in = sem("bias_in")
        xf_in = sem("xf_in")
        attn_in = sem("attn_in")
        xt_in = sem("xt_in")
        hm_in = sem("hm_in")
        w2_in = sem("w2_in")
        ffn_in = sem("ffn_in")
        zeroed = sem("zeroed")
        consts = sem("consts")
        cmax_done = sem("cmax_done")
        ones_done = sem("ones_done")
        cmax_row = sem("cmax_row")
        cpow_all = sem("cpow_all")
        cprep = sem("cprep")
        c_split = sem("c_split")
        bias_done = sem("bias_done")
        drive_done = sem("drive_done")
        gain_done = sem("gain_done")

        q_ready = [sem(f"q_ready{s}") for s in range(4)]
        act_ready = [q_ready[0]] + [sem(f"act_ready{s}") for s in range(1, 4)]
        clip_ready = sem("clip_ready")
        p_next_ready = sem("p_next_ready")
        hi_ready = [sem(f"hi_ready{s}") for s in range(4)]
        tanh_ready = [sem(f"tanh_ready{s}") for s in range(4)]
        lo_ready = [sem(f"lo_ready{s}") for s in range(4)]
        coupled = [sem(f"coupled{s}") for s in range(4)]
        square_ready = [sem(f"square_ready{s}") for s in range(4)]
        poly_ready = [sem(f"poly_ready{s}") for s in range(4)]
        base_ready = [sem(f"base_ready{s}") for s in range(4)]
        p_ready = [sem(f"p_ready{s}") for s in range(4)]
        drive_less_p_ready = sem("drive_less_p_ready")
        q_sum3_ready = sem("q_sum3_ready")
        q_drive_ready = sem("q_drive_ready")
        sums_ready = sem("sums_ready")
        drive_fed = sem("drive_fed")
        saved = sem("saved")

        w_hi_done = sem("w_hi_done")
        w_split = sem("w_split")
        folded = sem("folded")
        folded_out = sem("folded_out")
        km_done = sem("km_done")
        tq_ready = sem("tq_ready")
        tq_copied = sem("tq_copied")
        resid_done = sem("resid_done")
        stats_done = sem("stats_done")
        mv_done = sem("mv_done")
        var_done = sem("var_done")
        std_done = sem("std_done")
        rstd_done = sem("rstd_done")
        xn_done = sem("xn_done")
        xnt_psum = sem("xnt_psum")
        xnt_dve = sem("xnt_dve")
        xnt_act = sem("xnt_act")
        z_psum = sem("z_psum")
        z_dve = sem("z_dve")
        z_act = sem("z_act")
        vo_psum = sem("vo_psum")
        vo_dve = sem("vo_dve")
        vo_act = sem("vo_act")
        s_psum = sem("s_psum")
        sm_done = sem("sm_done")
        nmax_done = sem("nmax_done")
        ex_done = sem("ex_done")
        rinv_done = sem("rinv_done")
        ext_psum = sem("ext_psum")
        ext_dve = sem("ext_dve")
        ext_act = sem("ext_act")
        o_psum = sem("o_psum")
        x1_done = sem("x1_done")
        x1h_done = sem("x1h_done")
        z2_psum = sem("z2_psum")
        z2_act = sem("z2_act")
        vo2_psum = sem("vo2_psum")
        vo2_act = sem("vo2_act")
        s2_psum = sem("s2_psum")
        sm2_done = sem("sm2_done")
        nmax2_done = sem("nmax2_done")
        ex2_done = sem("ex2_done")
        inv2_done = sem("inv2_done")
        r2_done = sem("r2_done")
        ext2_psum = sem("ext2_psum")
        ext2_done = sem("ext2_done")
        h_psum = sem("h_psum")
        ht_hi_done = sem("ht_hi_done")
        h_done = sem("h_done")
        gu_psum = sem("gu_psum")
        silu_done = sem("silu_done")
        hid_done = sem("hid_done")
        hid_split = sem("hid_split")
        down_done = sem("down_done")
        y_psum = sem("y_psum")
        y_done = sem("y_done")
        out_done = sem("out_done")

        block = ctx.enter_context(nc.Block())

        @block.sync
        def _(sp):
            sp.dma_start(ct[:, :, :], coupling_t).then_inc(ct_in, 16)
            sp.dma_start(cf[:, :], cond_feat).then_inc(cond_in, 16)
            sp.dma_start(bias_sb[:, :], bias).then_inc(bias_in, 16)
            sp.dma_start(xf[:, :, :], x_feat).then_inc(xf_in, 16)
            for dst, src in ((wqt, wq_t), (wkt, wk_t), (wvt, wv_t), (wo_sb, wo)):
                sp.dma_start(dst[:, :, :], src).then_inc(attn_in, 16)
            for dst, src in ((gam, gamma), (bet, beta)):
                sp.dma_start(dst[:, :], src).then_inc(attn_in, 16)
            sp.dma_start(wq2[:, :], wq2_t).then_inc(w2_in, 16)
            sp.dma_start(wk2[:, :], wk2_t).then_inc(w2_in, 16)
            sp.dma_start(wo2_sb[:, :], wo2).then_inc(w2_in, 16)
            for h in range(HEADS):
                sp.dma_start(wv2[h * DK:(h + 1) * DK, :], wv2_t).then_inc(w2_in, 16)
            sp.dma_start(hm[:, :, :].rearrange("p b n -> p (b n)"),
                         cond_row.partition_broadcast(P)).then_inc(hm_in, 16)
            sp.dma_start(xt[:, :, :], x_tok).then_inc(xt_in, 16)
            sp.dma_start(w_ffn[:, 0:GATE_UP_COLS].rearrange("p (k o) -> p k o", k=NC),
                         w_gate_up_t).then_inc(ffn_in, 16)
            sp.dma_start(w_ffn[:, GATE_UP_COLS:W_COLS].rearrange("p (j n) -> p j n", j=NJ),
                         w_down_t).then_inc(ffn_in, 16)
            for b in range(B):
                sp.wait_ge(y_done, b + 1)
                sp.dma_start(out[b, :, :], yout[:, b, :]).then_inc(out_done, 16)
            sp.wait_ge(out_done, 16 * B)

        @block.gpsimd
        def _(pool):
            nc.gpsimd.memset(ident[:, :], 0.0).then_inc(zeroed, 1)
            nc.gpsimd.memset(causal[:, :], 0.0).then_inc(zeroed, 1)
            nc.gpsimd.memset(ones_row[:, :], 1.0).then_inc(ones_done, 1)
            pool.wait_ge(zeroed, 2)
            nc.gpsimd.affine_select(out=ident[:, :], in_=ident[:, :], compare_op=ALU.not_equal, fill=1.0,
                                    base=0, pattern=[[-1, P]], channel_multiplier=1).then_inc(consts, 1)
            nc.gpsimd.affine_select(out=causal[:, :], in_=causal[:, :], compare_op=ALU.is_ge, fill=MASKED,
                                    base=0, pattern=[[-1, T]], channel_multiplier=1).then_inc(consts, 1)
            pool.sem_inc(saved, 1)
            nc.gpsimd.memset(drive[:, T, :], 0.0).then_inc(drive_done, 1)
            pool.wait_ge(drive_done, 3)
            nc.gpsimd.tensor_copy(drive_now[:, :], drive[:, 0, :]).then_inc(drive_fed, 1)

            def step(t, between):
                pool.wait_ge(clip_ready, t + 1)
                pool.wait_ge(drive_fed, t + 1)
                nc.gpsimd.tensor_tensor(q_drive[:, :], q1[:, :], drive_now[:, :], ALU.add).then_inc(q_drive_ready, 1)
                nc.gpsimd.tensor_tensor(q_sum1[:, :], drive_now[:, :], q1[:, :], ALU.subtract)
                pool.wait_ge(q_drive_ready, t + 1)
                nc.gpsimd.tensor_tensor(q_2drive[:, :], q_drive[:, :], drive_now[:, :],
                                        ALU.add).then_inc(sums_ready, 1)
                pool.wait_ge(sums_ready, t + 1)
                pool.wait_ge(drive_less_p_ready, t + 1)
                nc.gpsimd.tensor_copy(drive_now[:, :], drive[:, bass.ds(t + 1, 1), :].rearrange("p a c -> p (a c)"))\
                    .then_inc(drive_fed, 1)
                between(t)
                pool.wait_ge(clip_ready, t + 2)
                nc.gpsimd.tensor_copy(trace[:, bass.ds(t, 1), :].rearrange("p a c -> p (a c)"),
                                      q1[:, :]).then_inc(saved, 1)

            def split_weights(t):
                piece = bass.ds((t - (T - SPLIT_STEPS)) * SPLIT_COLS, SPLIT_COLS)
                nc.gpsimd.tensor_copy(w_hi[:, piece], w_ffn[:, piece]).then_inc(w_hi_done, 1)
                pool.wait_ge(w_hi_done, t - (T - SPLIT_STEPS) + 1)
                nc.gpsimd.tensor_tensor(w_lo[:, piece], w_ffn[:, piece], w_hi[:, piece].bitcast(F32),
                                        ALU.subtract).then_inc(w_split, 1)

            with pool.Fori(0, T - SPLIT_STEPS) as t:
                step(t, lambda t: None)
            pool.wait_ge(ffn_in, 32)
            with pool.Fori(T - SPLIT_STEPS, T) as t:
                step(t, split_weights)
            pool.wait_ge(hm_in, 16)
            nc.gpsimd.tensor_scalar(km[:, :, :], hm[:, :, :], -1.0, 1.0, ALU.mult, ALU.add).then_inc(km_done, 1)
            pool.wait_ge(km_done, 1)
            nc.gpsimd.tensor_scalar(km[:, :, :], km[:, :, :], NEG, 1.0, ALU.mult, ALU.mult).then_inc(km_done, 1)
            pool.wait_ge(xt_in, 16)
            for i in range(4):
                pool.wait_ge(tq_copied, i + 1)
                nc.gpsimd.tensor_tensor(resid[:, 2 * i:2 * i + 2, :], xt[:, 2 * i:2 * i + 2, :],
                                        qtok[:, 2 * i:2 * i + 2, :], ALU.add).then_inc(resid_done, 1)

        @block.scalar
        def _(act):
            act.wait_ge(xf_in, 16)
            act.wait_ge(bias_done, 2)
            for c in range(NC):
                nc.scalar.activation(drive[:, 0:T, c * B:(c + 1) * B], xf[:, :, c * B:(c + 1) * B],
                                     ACT.Identity, bias=bias_d[:, c:c + 1],
                                     scale=0.5 * DT).then_inc(drive_done, 1)
            with act.Fori(0, T, UNROLL) as t0:
                count = [act.snap(t0 + k) for k in range(1, UNROLL + 1)]
                for now in count:
                    for s in range(4):
                        act.wait_ge(act_ready[s], now)
                        state = q_act if s else q[:, 0, :]
                        nc.scalar.activation(th_hi[:, :], state, ACT.Tanh).then_inc(hi_ready[s], 1)
                        nc.scalar.activation(th, state, ACT.Tanh).then_inc(tanh_ready[s], 1)
                        if s:
                            nc.scalar.activation(square[:, s, :], state, ACT.Square,
                                                 scale=CUBIC[s] ** 0.5).then_inc(square_ready[s], 1)

            nc.scalar.activation(sqrt_first[:, :], cscale[:, 0:1], ACT.Sqrt)
            for i in range(4):
                act.wait_ge(tq_ready, i + 1)
                nc.scalar.activation(qtok[:, 2 * i:2 * i + 2, :].rearrange("p a n -> p (a n)"),
                                     psum[:, i, :], ACT.Copy).then_inc(tq_copied, 1)
            act.wait_ge(var_done, 1)
            nc.scalar.activation(std[:, :], vare[:, :], ACT.Sqrt).then_inc(std_done, 1)
            act.wait_ge(folded, 1)
            nc.scalar.activation(wqk[:, :, :].rearrange("p c n -> p (c n)"), psum[:, 0, :],
                                 ACT.Copy).then_inc(folded_out, 1)
            act.wait_ge(w_split, SPLIT_STEPS)
            act.wait_ge(attn_in, 16 * 6)
            for i in range(2):
                act.wait_ge(xnt_psum, i + 1)
                nc.scalar.activation(xnt[:, 1, i * HALF:(i + 1) * HALF], psum[:, 6 + i, :], ACT.Identity,
                                     bias=bet[:, 1:2], scale=gam[:, 1:2]).then_inc(xnt_act, 1)
            act.wait_ge(folded, 2)
            nc.scalar.activation(wvo[:, :, :].rearrange("p c n -> p (c n)"), psum[:, 4, :],
                                 ACT.Copy).then_inc(folded_out, 1)
            act.wait_ge(folded, 3)
            nc.scalar.activation(a2[:, :], psum[:, 5, 0:P], ACT.Copy, scale=DK ** -0.5)
            nc.scalar.activation(wvo2[:, :], psum[:, 5, P:2 * P], ACT.Copy).then_inc(folded_out, 1)
            for i in range(2):
                act.wait_ge(z_psum, 2 * i + 2)
                nc.scalar.activation(z[:, 1, i * HALF:(i + 1) * HALF], psum[:, 2 + i, :],
                                     ACT.Copy).then_inc(z_act, 1)

            def values_out(i):
                act.wait_ge(vo_psum, 2 * i + 2)
                nc.scalar.activation(vo[:, 4 * i + 2:4 * i + 4, :].rearrange("p a n -> p (a n)"),
                                     psum[:, 5 + 2 * i, :], ACT.Copy).then_inc(vo_act, 1)

            for i in range(2):
                for b in range(4 * i, 4 * i + 4):
                    act.wait_ge(nmax_done, i + 1)
                    nc.scalar.activation(ex[:, b, :], sm[:, b, :], ACT.Exp, bias=nmax[:, b:b + 1],
                                         accum_out=rsum[:, b:b + 1]).then_inc(ex_done, 1)
                values_out(i)
            act.wait_ge(ext_psum, 2)
            nc.scalar.activation(ext[:, 4:8, :].rearrange("p a n -> p (a n)"), psum[:, 3, :],
                                 ACT.Copy).then_inc(ext_act, 1)
            for i in range(4):
                act.wait_ge(z2_psum, i + 1)
                nc.scalar.activation(z2[:, 2 * i:2 * i + 2, :].rearrange("p a n -> p (a n)"),
                                     psum[:, i, :], ACT.Copy).then_inc(z2_act, 1)

            def values2_out(i):
                act.wait_ge(vo2_psum, i + 1)
                nc.scalar.activation(vo2[:, 2 * i:2 * i + 2, :, :].rearrange("p a c n -> p (a c n)"),
                                     psum[:, 4 + i, :], ACT.Copy).then_inc(vo2_act, 1)

            def turned_out(b):
                act.wait_ge(ext2_psum, b + 1)
                if b >= 2:
                    act.wait_ge(h_psum, b - 1)
                nc.scalar.activation(ext2[:, b % 2, :, :].rearrange("p c n -> p (c n)"), psum[:, 2, :],
                                     ACT.Copy).then_inc(ext2_done, 1)

            for b in range(B):
                act.wait_ge(nmax2_done, b + 1)
                if b >= 2:
                    act.wait_ge(ext2_psum, b - 1)
                for c in range(NC):
                    nc.scalar.activation(ex2[:, b % 2, c, :], sm2[:, b % 2, c, :], ACT.Exp,
                                         bias=nmax2[:, b, c:c + 1],
                                         accum_out=sum2[:, b, c:c + 1]).then_inc(ex2_done, 1)
                if b >= 1:
                    turned_out(b - 1)
                if b < 4:
                    values2_out(b)
            turned_out(B - 1)
            for n in range(2 * NJ):
                act.wait_ge(gu_psum, n + 1)
                if n >= 2:
                    act.wait_ge(hid_done, 2 * n - 2)
                nc.scalar.activation(sg[:, n % 2, :], psum[:, 4 + 2 * (n % 2), :], ACT.Silu).then_inc(silu_done, 1)

        @block.vector
        def _(dve):
            stt = nc.vector.scalar_tensor_tensor
            dve.wait_ge(ct_in, 16)
            nc.vector.reduce_max(cmax[:, :], ct[:, :, :].rearrange("p c n -> p (c n)"), AX_X,
                                 apply_absolute_value=True).then_inc(cmax_done, 1)
            dve.wait_ge(bias_in, 16)
            nc.vector.tensor_scalar(bias_d[:, :], bias_sb[:, :], -P_SHIFT, 0.5 * DT, ALU.add,
                                    ALU.mult).then_inc(bias_done, 2)
            dve.wait_ge(cmax_row, 1)
            nc.vector.reduce_max(call[:, :], psum[0:1, 3, 0:P], AX_X).then_inc(cprep, 1)
            dve.wait_ge(cprep, 1)
            nc.vector.tensor_scalar(cclip[:, :], call[:, :], 2.0 ** -100, None, ALU.max).then_inc(cprep, 1)
            dve.wait_ge(cprep, 2)
            nc.vector.tensor_scalar(cpow[:, 0:1].bitcast(U32), cclip[:, :].bitcast(U32), EXPONENT, None,
                                    ALU.bitwise_and).then_inc(cprep, 1)
            nc.vector.tensor_scalar(cpow[:, 1:2].bitcast(U32), cclip[:, :].bitcast(U32), EXPONENT, EXPONENT,
                                    ALU.bitwise_and, ALU.bitwise_xor).then_inc(cprep, 1)
            dve.wait_ge(cpow_all, 1)
            nc.vector.tensor_copy(cscale[:, :], psum[:, 4, 0:2]).then_inc(cprep, 1)
            dve.wait_ge(cprep, 5)
            nc.vector.tensor_scalar(cscaled[:, :, :], ct[:, :, :], cscale[:, 1:2], 2.0 ** 12, ALU.mult,
                                    ALU.mult).then_inc(cprep, 1)
            for s in range(4):
                nc.vector.tensor_scalar(gain[:, s:s + 1], cscale[:, 0:1], STEP[s] * 2.0 ** -13, None,
                                        ALU.mult).then_inc(gain_done, 1)
            dve.wait_ge(cprep, 6)
            nc.vector.tensor_copy(c_hi[:, :, :], cscaled[:, :, :]).then_inc(cprep, 1)
            dve.wait_ge(cprep, 7)
            nc.vector.tensor_tensor(c_lo[:, :, :], cscaled[:, :, :], c_hi[:, :, :],
                                    ALU.subtract).then_inc(c_split, 1)
            dve.wait_ge(cond_in, 16)
            nc.vector.tensor_scalar(p1[:, :], cf[:, :], -P_SHIFT, None, ALU.add).then_inc(p_ready[0], 1)
            nc.vector.tensor_copy(q1[:, :], cf[:, :]).then_inc(clip_ready, 1)
            dve.sem_inc(p_next_ready, 1)
            nc.vector.tensor_copy(q[:, 0, :], cf[:, :]).then_inc(q_ready[0], 1)
            dve.wait_ge(gain_done, 4)
            dve.wait_ge(drive_fed, 1)

            def axpy(dst, a, scalar, b, op1=ALU.add):
                return stt(out=dst, in0=a, scalar=scalar, in1=b, op0=ALU.mult, op1=op1)

            def cubic(s, qs, now):
                dve.wait_ge(square_ready[s], now)
                stt(out=poly[:, s, :], in0=square[:, s, :], scalar=LINEAR[s], in1=qs, op0=ALU.subtract,
                    op1=ALU.mult).then_inc(poly_ready[s], 1)

            def split_tanh(s, now):
                dve.wait_ge(tanh_ready[s], now)
                nc.vector.tensor_tensor(th_lo[:, :], th, th_hi[:, :], ALU.subtract).then_inc(lo_ready[s], 1)

            def sum_base(s, linear, now):
                dve.wait_ge(poly_ready[s], now)
                axpy(base[:, s, :], linear, 1.0 / 3.0 if s == 3 else 1.0, poly[:, s, :],
                     ALU.subtract).then_inc(base_ready[s], 1)

            def add_coupling(s, now):
                dve.wait_ge(coupled[s], now)
                following = (s + 1) % 4
                copies = [(q[:, following, :], q_ready[following])]
                if following:
                    copies.insert(0, (q_act, act_ready[following]))
                for dst, ready in copies:
                    stt(out=dst.rearrange("p (c b) -> p c b", c=NC), in0=coupling_sum[:, s % 2, 0:NC, 0:B],
                        scalar=gain[:, s:s + 1], in1=base[:, s, :].rearrange("p (c b) -> p c b", c=NC),
                        op0=ALU.mult, op1=ALU.add).then_inc(ready, 1)

            with dve.Fori(0, T, UNROLL) as t0:
                count = [dve.snap(t0 + k) for k in range(1, UNROLL + 2)]
                for now, after in zip(count, count[1:]):
                    dve.wait_ge(p_ready[0], now)
                    axpy(drive_less_p[:, :], p1[:, :], -0.5 * DT, drive_now[:, :]).then_inc(drive_less_p_ready, 1)
                    dve.wait_ge(clip_ready, now)
                    stt(out=square[:, 0, :], in0=q1[:, :], scalar=CUBIC[0], in1=q1[:, :], op0=ALU.mult,
                        op1=ALU.mult).then_inc(square_ready[0], 1)
                    split_tanh(0, now)
                    cubic(0, q1[:, :], now)
                    axpy(rate[:, 0, :], p1[:, :], -BETA, q1[:, :])
                    sum_base(0, drive_less_p[:, :], now)
                    nc.vector.tensor_tensor(affine[:, 0, :], drive_less_p[:, :], q1[:, :], ALU.add)
                    dve.wait_ge(base_ready[0], now)
                    axpy(p2[:, :], rate[:, 0, :], E2, p1[:, :]).then_inc(p_ready[1], 1)
                    add_coupling(0, now)
                    dve.wait_ge(p_ready[1], now)
                    axpy(affine[:, 1, :], rate[:, 0, :], -0.5 * DT * E2, affine[:, 0, :])
                    dve.wait_ge(q_ready[1], now)
                    axpy(rate[:, 1, :], p2[:, :], -BETA, q[:, 1, :])
                    split_tanh(1, now)
                    cubic(1, q[:, 1, :], now)
                    axpy(p_sum1[:, :], rate[:, 0, :], DT * EPS_P / 6.0, p1[:, :])
                    sum_base(1, affine[:, 1, :], now)
                    dve.wait_ge(sums_ready, now)
                    axpy(p3[:, :], rate[:, 1, :], E2, p1[:, :]).then_inc(p_ready[2], 1)
                    dve.wait_ge(base_ready[1], now)
                    nc.vector.tensor_tensor(q_sum2[:, :], q_sum1[:, :], q[:, 1, :], ALU.add)
                    add_coupling(1, now)
                    dve.wait_ge(p_ready[2], now)
                    axpy(affine[:, 2, :], p3[:, :], -DT, q_2drive[:, :])
                    dve.wait_ge(q_ready[2], now)
                    axpy(rate[:, 2, :], p3[:, :], -BETA, q[:, 2, :])
                    split_tanh(2, now)
                    cubic(2, q[:, 2, :], now)
                    dve.wait_ge(drive_fed, after)
                    axpy(p_sum2[:, :], rate[:, 1, :], DT * EPS_P / 3.0, p_sum1[:, :])
                    sum_base(2, affine[:, 2, :], now)
                    axpy(p4[:, :], rate[:, 2, :], 2.0 * E2, p1[:, :]).then_inc(p_ready[3], 1)
                    dve.wait_ge(base_ready[2], now)
                    axpy(q_sum3[:, :], q[:, 2, :], 2.0, q_sum2[:, :]).then_inc(q_sum3_ready, 1)
                    add_coupling(2, now)
                    dve.wait_ge(q_sum3_ready, now)
                    axpy(affine[:, 3, :], p4[:, :], -0.5 * DT, q_sum3[:, :])
                    dve.wait_ge(q_ready[3], now)
                    axpy(rate[:, 3, :], p4[:, :], -BETA, q[:, 3, :])
                    split_tanh(3, now)
                    cubic(3, q[:, 3, :], now)
                    dve.wait_ge(saved, now)
                    axpy(p_sum3[:, :], rate[:, 2, :], DT * EPS_P / 3.0, p_sum2[:, :])
                    sum_base(3, affine[:, 3, :], now)
                    dve.wait_ge(base_ready[3], now)
                    axpy(p_next[:, :], rate[:, 3, :], DT * EPS_P / 6.0, p_sum3[:, :]).then_inc(p_next_ready, 1)
                    add_coupling(3, now)
                    dve.wait_ge(p_next_ready, after)
                    nc.vector.tensor_scalar(p1[:, :], p_next[:, :], -CLAMP - P_SHIFT, CLAMP - P_SHIFT, ALU.max,
                                            ALU.min).then_inc(p_ready[0], 1)
                    dve.wait_ge(q_ready[0], after)
                    nc.vector.tensor_scalar(q1[:, :], q[:, 0, :], -CLAMP, CLAMP, ALU.max,
                                            ALU.min).then_inc(clip_ready, 1)

            for b in range(B):
                dve.wait_ge(tq_copied, b // 2 + 1)
                nc.vector.bn_stats(stats[:, b, :], qtok[:, b, :]).then_inc(stats_done, 1)
            for b in range(B):
                dve.wait_ge(stats_done, b + 1)
                nc.vector.bn_aggr(mv[:, b, :], stats[:, b, :]).then_inc(mv_done, 1)
            dve.wait_ge(mv_done, B)
            nc.vector.tensor_scalar(vare[:, :], mv[:, :, 1], LN_EPS, None, ALU.add).then_inc(var_done, 1)
            dve.wait_ge(std_done, 1)
            nc.vector.reciprocal(rstd[:, :], std[:, :]).then_inc(rstd_done, 1)
            dve.wait_ge(rstd_done, 1)
            for b in range(B):
                nc.vector.tensor_scalar(xn[:, b, :], qtok[:, b, :], mv[:, b, 0:1], rstd[:, b:b + 1],
                                        ALU.subtract, ALU.mult).then_inc(xn_done, 1)
            dve.wait_ge(w_split, SPLIT_STEPS)
            dve.wait_ge(attn_in, 16 * 6)
            for i in range(2):
                dve.wait_ge(xnt_psum, i + 1)
                nc.vector.tensor_scalar(xnt[:, 0, i * HALF:(i + 1) * HALF], psum[:, 4 + i, :], gam[:, 0:1],
                                        bet[:, 0:1], ALU.mult, ALU.add).then_inc(xnt_dve, 1)
            for i in range(2):
                dve.wait_ge(z_psum, 2 * i + 1)
                nc.vector.tensor_copy(z[:, 0, i * HALF:(i + 1) * HALF], psum[:, i, :]).then_inc(z_dve, 1)
            dve.wait_ge(consts, 2)
            for i in range(2):
                dve.wait_ge(s_psum, i + 1)
                stt(out=sm[:, 4 * i:4 * i + 4, :], in0=psum[:, i, :].rearrange("p (a n) -> p a n", a=4),
                    scalar=float(N) ** -0.5, in1=causal[:, None, :].to_broadcast([P, 4, T]), op0=ALU.mult,
                    op1=ALU.add).then_inc(sm_done, 1)
                dve.wait_ge(sm_done, i + 1)
                nc.vector.tensor_reduce(nmax[:, 4 * i:4 * i + 4], sm[:, 4 * i:4 * i + 4, :], AX_X, ALU.max,
                                        negate=True).then_inc(nmax_done, 1)
            for i in range(2):
                dve.wait_ge(vo_psum, 2 * i + 1)
                nc.vector.tensor_copy(vo[:, 4 * i:4 * i + 2, :].rearrange("p a n -> p (a n)"),
                                      psum[:, 4 + 2 * i, :]).then_inc(vo_dve, 1)
            dve.wait_ge(ex_done, B)
            nc.vector.reciprocal(rinv[:, :], rsum[:, :]).then_inc(rinv_done, 1)
            dve.wait_ge(ext_psum, 1)
            nc.vector.tensor_copy(ext[:, 0:4, :].rearrange("p a n -> p (a n)"), psum[:, 2, :]).then_inc(ext_dve, 1)
            dve.wait_ge(rinv_done, 1)
            dve.wait_ge(resid_done, 4)
            for b in range(B):
                dve.wait_ge(o_psum, b // 2 + 1)
                stt(out=x1[:, b, :], in0=psum[:, 4 + b // 2, (b % 2) * N:(b % 2 + 1) * N], scalar=rinv[:, b:b + 1],
                    in1=resid[:, b, :], op0=ALU.mult, op1=ALU.add).then_inc(x1_done, 1)
            dve.wait_ge(hm_in, 16)
            for b in range(B):
                dve.wait_ge(x1_done, b + 1)
                nc.vector.tensor_tensor(x1h[:, b, :], x1[:, b, :], hm[:, b, :], ALU.mult).then_inc(x1h_done, 1)

            dve.wait_ge(km_done, 2)

            def masked_max(b):
                dve.wait_ge(s2_psum, b + 1)
                if b >= 2:
                    dve.wait_ge(ex2_done, 2 * (b - 1))
                for c in range(NC):
                    nc.vector.tensor_tensor_reduce(out=sm2[:, b % 2, c, :], in0=psum[:, b % 2, c * N:(c + 1) * N],
                                                   in1=km[:, b, :], scale=1.0, scalar=MASKED, op0=ALU.add,
                                                   op1=ALU.max, accum_out=max2[:, b, c:c + 1]).then_inc(sm2_done, 1)
                dve.wait_ge(sm2_done, 2 * (b + 1))
                nc.vector.tensor_scalar(nmax2[:, b, :], max2[:, b, :], -1.0, None, ALU.mult).then_inc(nmax2_done, 1)

            def over_sum(b):
                dve.wait_ge(ex2_done, 2 * (b + 1))
                nc.vector.reciprocal(inv2[:, b, :], sum2[:, b, :]).then_inc(inv2_done, 1)
                dve.wait_ge(inv2_done, b + 1)
                nc.vector.tensor_tensor(r2[:, b, :], inv2[:, b, :],
                                        cf[:, :].rearrange("p (c b) -> p b c", c=NC)[:, b, :],
                                        ALU.mult).then_inc(r2_done, 1)

            def weighed(b):
                dve.wait_ge(h_psum, b + 1)
                dve.wait_ge(r2_done, b + 1)
                nc.vector.tensor_tensor(ht_hi[:, :, b * P:(b + 1) * P],
                                        psum[:, 3, 0:2 * P].rearrange("p (c e) -> p c e", c=NC),
                                        r2[:, b, :, None].to_broadcast([P, NC, P]), ALU.mult).then_inc(ht_hi_done, 1)
                dve.wait_ge(ht_hi_done, b + 1)
                for c in range(NC):
                    last = stt(out=ht_lo[:, c, b * P:(b + 1) * P], in0=psum[:, 3, c * P:(c + 1) * P],
                               scalar=r2[:, b, c:c + 1], in1=ht_hi[:, c, b * P:(b + 1) * P].bitcast(F32),
                               op0=ALU.mult, op1=ALU.subtract)
                last.then_inc(h_done, 1)

            def gated(n):
                dve.wait_ge(silu_done, n + 1)
                if n == NJ + 2:
                    dve.wait_ge(y_psum, B // 2)
                elif n >= 3:
                    dve.wait_ge(down_done, n - 2 if n < NJ + 2 else n - 3)
                nc.vector.tensor_tensor(hid_hi[:, n % 3, :], sg[:, n % 2, :],
                                        psum[:, 5 + 2 * (n % 2), :], ALU.mult).then_inc(hid_done, 1)
                nc.vector.tensor_tensor(hid[:, n % 2, :], sg[:, n % 2, :],
                                        psum[:, 5 + 2 * (n % 2), :], ALU.mult).then_inc(hid_done, 1)
                dve.wait_ge(hid_done, 2 * n + 2)
                nc.vector.tensor_tensor(hid_lo[:, n % 3, :], hid[:, n % 2, :], hid_hi[:, n % 3, :].bitcast(F32),
                                        ALU.subtract).then_inc(hid_split, 1)

            def finish(b):
                dve.wait_ge(y_psum, b + 1)
                nc.vector.tensor_tensor(yout[:, b, :], psum[:, b % 4, 0:N],
                                        x1[:, b, :], ALU.add).then_inc(y_done, 1)

            masked_max(0)
            masked_max(1)
            for b in range(B):
                over_sum(b)
                if b + 2 < B:
                    masked_max(b + 2)
                weighed(b)
            for n in range(2 * NJ):
                gated(n)
                if n == NJ + 1:
                    for b in range(B // 2):
                        finish(b)
            for b in range(B // 2, B):
                finish(b)

        @block.tensor
        def _(pe):
            mm = nc.tensor.matmul
            pe.wait_ge(consts, 1)
            pe.wait_ge(cmax_done, 1)
            nc.tensor.transpose(psum[0:1, 3, 0:P], cmax[:, :], ident[:, :]).then_inc(cmax_row, 1)
            pe.wait_ge(ones_done, 1)
            pe.wait_ge(cprep, 4)
            mm(psum[:, 4, 0:2], ones_row[:, :], cpow[:, :], start=True, stop=True).then_inc(cpow_all, 1)
            pe.wait_ge(c_split, 1)

            def couple(s, m, part, th_part, start, stop):
                for k in range(NC):
                    last = mm(coupling_sum[:, s % 2, m, 0:B], part[:, k, m * P:(m + 1) * P],
                              th_part[:, k * B:(k + 1) * B], start=(start and k == 0), stop=(stop and k == NC - 1))
                return last

            with pe.Fori(0, T, UNROLL) as t0:
                count = [pe.snap(t0 + k) for k in range(1, UNROLL + 1)]
                for now in count:
                    for s in range(4):
                        pe.wait_ge(hi_ready[s], now)
                        for m in range(NC):
                            couple(s, m, c_hi, th_hi, True, False)
                            couple(s, m, c_lo, th_hi, False, False)
                        pe.wait_ge(lo_ready[s], now)
                        for m in range(NC):
                            last = couple(s, m, c_hi, th_lo, False, True)
                        last.then_inc(coupled[s], 1)

            pe.wait_ge(saved, T + 1)
            pe.wait_ge(q_ready[0], T + 1)
            for b in range(B):
                for c in range(NC):
                    last = nc.tensor.transpose(psum[:, b // 2, (b % 2) * N + c * P:(b % 2) * N + (c + 1) * P],
                                               trace[:, :, c * B + b], ident[:, :])
                if b % 2:
                    last.then_inc(tq_ready, 1)

            def fold(bank, left, right):
                for m in range(NC):
                    for k in range(NC):
                        last = mm(psum[:, bank, m * N:(m + 1) * N], left[:, k, m * P:(m + 1) * P], right[:, k, :],
                                  start=(k == 0), stop=(k == NC - 1))
                last.then_inc(folded, 1)

            pe.wait_ge(attn_in, 16 * 6)
            pe.wait_ge(tq_copied, 1)
            fold(0, wqt, wkt)
            for b in range(B):
                pe.wait_ge(xn_done, b + 1)
                for c in range(NC):
                    last = nc.tensor.transpose(psum[:, 4 + 2 * c + b // 4, (b % 4) * P:(b % 4 + 1) * P],
                                               xn[:, b, c * P:(c + 1) * P], ident[:, :])
                if b % 4 == 3:
                    last.then_inc(xnt_psum, 1)
            pe.wait_ge(xnt_dve, 1)
            fold(4, wvt, wo_sb)
            pe.wait_ge(xnt_dve, 2)
            pe.wait_ge(w2_in, 16 * (3 + HEADS))
            mm(psum[:, 5, 0:P], wq2[:, :], wk2[:, :], start=True, stop=True)
            mm(psum[:, 5, P:2 * P], wv2[:, :], wo2_sb[:, :], start=True, stop=True).then_inc(folded, 1)
            pe.wait_ge(tq_copied, 4)
            pe.wait_ge(folded_out, 1)
            for i in range(2):
                pe.wait_ge(xnt_act, i + 1)
                for m in range(NC):
                    for k in range(NC):
                        last = mm(psum[:, 2 * m + i, :], wqk[:, k, m * P:(m + 1) * P],
                                  xnt[:, k, i * HALF:(i + 1) * HALF], start=(k == 0), stop=(k == NC - 1))
                    last.then_inc(z_psum, 1)

            def values(b):
                for k in range(NC):
                    last = mm(psum[:, 4 + b // 2, (b % 2) * N:(b % 2 + 1) * N], xnt[:, k, b * P:(b + 1) * P],
                              wvo[:, k, :], start=(k == 0), stop=(k == NC - 1))
                if b % 2:
                    last.then_inc(vo_psum, 1)

            pe.wait_ge(folded_out, 3)
            values(0)
            values(1)
            for b in range(B):
                if b % 4 == 0:
                    pe.wait_ge(z_dve, b // 4 + 1)
                    pe.wait_ge(z_act, 2)
                for k in range(NC):
                    last = mm(psum[:, b // 4, (b % 4) * T:(b % 4 + 1) * T], z[:, k, b * P:(b + 1) * P],
                              xnt[:, k, b * P:(b + 1) * P], start=(k == 0), stop=(k == NC - 1))
                if b % 4 == 3:
                    last.then_inc(s_psum, 1)
            for b in range(2, B):
                values(b)
            for b in range(B):
                pe.wait_ge(ex_done, b + 1)
                last = nc.tensor.transpose(psum[:, 2 + b // 4, (b % 4) * T:(b % 4 + 1) * T], ex[:, b, :], ident[:, :])
                if b % 4 == 3:
                    last.then_inc(ext_psum, 1)
            pe.wait_ge(vo_dve, 2)
            pe.wait_ge(vo_act, 2)
            for b in range(B):
                if b % 4 == 0:
                    pe.wait_ge((ext_dve, ext_act)[b // 4], 1)
                last = mm(psum[:, 4 + b // 2, (b % 2) * N:(b % 2 + 1) * N], ext[:, b, :], vo[:, b, :],
                          start=True, stop=True)
                if b % 2:
                    last.then_inc(o_psum, 1)
            pe.wait_ge(sm_done, 2)
            for i in range(4):
                pe.wait_ge(x1_done, 2 * i + 2)
                mm(psum[:, i, :], a2[:, :], x1[:, 2 * i:2 * i + 2, :].rearrange("p a n -> p (a n)"),
                   start=True, stop=True).then_inc(z2_psum, 1)

            def scores2(b):
                if b < 2:
                    pe.wait_ge(z2_act, b + 1)
                else:
                    pe.wait_ge(z2_act, b // 2 + 1)
                    pe.wait_ge(sm2_done, 2 * (b - 1))
                pe.wait_ge(x1h_done, b + 1)
                for c in range(NC):
                    last = mm(psum[:, b % 2, c * N:(c + 1) * N], z2[:, b, c * P:(c + 1) * P], x1h[:, b, :],
                              start=True, stop=True)
                last.then_inc(s2_psum, 1)

            def turn2(b):
                pe.wait_ge(ex2_done, 2 * b + 2)
                if b >= 1:
                    pe.wait_ge(ext2_done, b)
                for c in range(NC):
                    for k in range(NC):
                        last = nc.tensor.transpose(psum[:, 2, k * N + c * P:k * N + (c + 1) * P],
                                                   ex2[:, b % 2, c, k * P:(k + 1) * P], ident[:, :])
                last.then_inc(ext2_psum, 1)

            def weigh2(b):
                pe.wait_ge(ext2_done, b + 1)
                pe.wait_ge(vo2_act, b // 2 + 1)
                if b:
                    pe.wait_ge(h_done, b)
                for c in range(NC):
                    for k in range(NC):
                        last = mm(psum[:, 3, c * P:(c + 1) * P], ext2[:, b % 2, k, c * P:(c + 1) * P],
                                  vo2[:, b, k, :], start=(k == 0), stop=(k == NC - 1))
                last.then_inc(h_psum, 1)

            def mm_parts(dst, left, right, first, stop):
                mm(dst, left[0], right[0], start=first, stop=False)
                mm(dst, left[0], right[1], start=False, stop=False)
                return mm(dst, left[1], right[0], start=False, stop=stop)

            def gate_and_up(n):
                j, half = n % NJ, n // NJ
                if n == 0:
                    pe.wait_ge(w_split, SPLIT_STEPS)
                    pe.wait_ge(vo2_act, 4)
                    pe.wait_ge(h_done, B // 2)
                if n >= 2:
                    pe.wait_ge(hid_done, 2 * n - 2)
                cols = slice(half * HALF, (half + 1) * HALF)
                for gu in range(2):
                    rows = slice(gu * INTER + j * P, gu * INTER + (j + 1) * P)
                    for k in range(NC):
                        last = mm_parts(psum[:, 4 + 2 * (n % 2) + gu, :], [part[:, k, rows] for part in gate_up],
                                        (ht_hi[:, k, cols], ht_lo[:, k, cols]), k == 0, k == NC - 1)
                last.then_inc(gu_psum, 1)

            scores2(0)
            scores2(1)
            pe.wait_ge(x1_done, B)
            for b in range(B):
                for c in range(NC):
                    last = mm(psum[:, 4 + b // 2, (b % 2) * N + c * P:(b % 2) * N + (c + 1) * P],
                              x1[:, b, c * P:(c + 1) * P], wvo2[:, :], start=True, stop=True)
                if b % 2:
                    last.then_inc(vo2_psum, 1)
            for b in range(B - 1):
                turn2(b)
                if b + 2 < B:
                    scores2(b + 2)
                weigh2(b)
            turn2(B - 1)
            gate_and_up(0)
            weigh2(B - 1)
            gate_and_up(1)

            def down_products(n):
                j, half = n % NJ, n // NJ
                pe.wait_ge(hid_split, n + 1)
                for b in range(4):
                    if n == NJ:
                        pe.wait_ge(y_done, b + 1)
                    rows = slice(b * P, (b + 1) * P)
                    last = mm_parts(psum[:, b, 0:N], (hid_hi[:, n % 3, rows], hid_lo[:, n % 3, rows]),
                                    [part[:, j, :] for part in down], j == 0, j == NJ - 1)
                    if j == NJ - 1:
                        last.then_inc(y_psum, 1)
                    elif b == 3:
                        last.then_inc(down_done, 1)

            pe.wait_ge(h_done, B)
            for n in range(2, 2 * NJ):
                gate_and_up(n)
                down_products(n - 2)
            down_products(2 * NJ - 2)
            down_products(2 * NJ - 1)


def kernel(x, cond_2048, L0_cond_coupling, L0_cond_bias, L0_attn_qkv, L0_attn_o_proj, L0_attn_gamma,
           L0_attn_beta, L0_cond2_Wq, L0_cond2_Wk, L0_cond2_Wv, L0_cond2_Wo, L0_ffn_w_gate_up, L0_ffn_w_down):
    import numpy as np
    import concourse.bacc as bacc
    from concourse.bass_utils import run_bass_kernel_spmd

    def chunks(a):
        a = np.asarray(a)
        a = a.reshape(a.shape[0] // P, P, *a.shape[1:])
        return np.ascontiguousarray(np.moveaxis(a, 0, 1))

    x = np.asarray(x)
    cond = np.asarray(cond_2048)
    qkv = np.asarray(L0_attn_qkv)
    arrays = {
        "x_feat": np.ascontiguousarray(x.reshape(B, T, NC, P).transpose(3, 1, 2, 0).reshape(P, T, COLS)),
        "x_tok": np.ascontiguousarray(x.transpose(1, 0, 2)),
        "cond_feat": np.ascontiguousarray(cond.reshape(B, NC, P).transpose(2, 1, 0).reshape(P, COLS)),
        "cond_row": np.ascontiguousarray(cond.reshape(B * N)),
        "coupling_t": chunks(np.asarray(L0_cond_coupling).T),
        "bias": chunks(L0_cond_bias),
        "wq_t": chunks(qkv[:, 0:N].T),
        "wk_t": chunks(qkv[:, N:2 * N].T),
        "wv_t": chunks(qkv[:, 2 * N:3 * N].T),
        "wo": chunks(L0_attn_o_proj),
        "gamma": chunks(L0_attn_gamma),
        "beta": chunks(L0_attn_beta),
        "wq2_t": np.ascontiguousarray(np.asarray(L0_cond2_Wq)[1].T),
        "wk2_t": np.ascontiguousarray(np.asarray(L0_cond2_Wk)[1].T),
        "wv2_t": np.ascontiguousarray(np.asarray(L0_cond2_Wv)[1].T),
        "wo2": np.ascontiguousarray(np.asarray(L0_cond2_Wo)),
        "w_gate_up_t": chunks(np.asarray(L0_ffn_w_gate_up).T),
        "w_down_t": chunks(np.asarray(L0_ffn_w_down).T),
    }
    nc = bacc.Bacc("TRN2", target_bir_lowering=False, num_devices=1)
    args = [nc.dram_tensor(f"in_{k}", a.shape, mybir.dt.from_np(a.dtype), kind="ExternalInput").ap()
            for k, a in arrays.items()]
    out = nc.dram_tensor("out_y", (B, T, N), F32, kind="ExternalOutput").ap()
    fhn_attention_ffn(nc, *args, out)
    result = run_bass_kernel_spmd(nc, [{f"in_{k}": a for k, a in arrays.items()}], core_ids=[0])
    return result.results[0]["out_y"]
```
